# Optimizing a Trainium2 kernel written in Bass

```python
import numpy as np
import jax
import jax.numpy as jnp

def _softmax(x, axis=-1):
    return jax.nn.softmax(x, axis=axis)

def _gelu(x):
    return jax.nn.gelu(x, approximate=True)

def _silu(x):
    return jax.nn.silu(x)

def _sigmoid(x):
    return jax.nn.sigmoid(x)

def _layernorm(x, axis=-1, eps=1e-05):
    m = jnp.mean(x, axis=axis, keepdims=True)
    v = jnp.var(x, axis=axis, keepdims=True)
    return (x - m) / jnp.sqrt(v + eps)

def _scatter_add(tgt, idx, src, axis=0):
    return tgt.at[idx].add(src)

def _segment_sum(src, seg, n):
    return jax.ops.segment_sum(src, seg, n)
kernel_name = 'mk_seq_preln_d1_jaxref_r8_ca53f6'

def setup_inputs(seed: int=0):
    np.random.seed(seed)
    _w = jnp.asarray

    def _L0_attn_setup():
        import jax, jax.numpy as jnp
        import numpy as np
        B, N, D, H = (2, 256, 128, 16)
        HD = D // H
        SCALING = (D / H) ** 0.5
        EPS = 1e-05
        key = jax.random.key(seed)
        k1, k2, k3 = jax.random.split(key, 3)
        return {'z': jax.random.normal(k1, (B, N, D), dtype=jnp.float32), 'ln_scale': jnp.ones((D,), dtype=jnp.float32), 'ln_bias': jnp.zeros((D,), dtype=jnp.float32), 'w_qkv': jax.random.normal(k2, (D, 3 * D), dtype=jnp.float32) * D ** (-0.5), 'w_proj': jax.random.normal(k3, (D, D), dtype=jnp.float32) * D ** (-0.5), 'b_proj': jnp.zeros((D,), dtype=jnp.float32)}
    _L0_attn_in = _L0_attn_setup()

    def _L0_ffn_setup():
        import jax, jax.numpy as jnp
        import numpy as np
        DIM = 128
        HEADS = 16
        HD = DIM // HEADS
        M = 32
        E = 4
        K = 2
        HID = 256
        MID = 256
        LB = 0.01
        EPS = 1.1920929e-07

        def _rms(x, w):
            return x * jax.lax.rsqrt(jnp.mean(x * x, axis=-1, keepdims=True) + EPS) * w

        def _gelu(x):
            return jax.nn.gelu(x, approximate=False)
        key = jax.random.key(seed)
        ks = jax.random.split(key, 20)
        d = DIM
        w = lambda k, s: jax.random.normal(k, s, jnp.float32) * 0.02
        return {'x': jax.random.normal(ks[0], (4, 128, d), jnp.float32), 'n1_w': jnp.ones((d,), jnp.float32), 'n2_w': jnp.ones((d,), jnp.float32), 'wq': w(ks[1], (d, d)), 'wk': w(ks[2], (d, d)), 'wv': w(ks[3], (d, d)), 'wo': w(ks[4], (d, d)), 'qn_w': jnp.ones((HD,), jnp.float32), 'kn_w': jnp.ones((HD,), jnp.float32), 'gate_w': w(ks[5], (E, d)), 'e0_up': w(ks[6], (HID, d)), 'e0_down': w(ks[7], (d, HID)), 'e1_w1': w(ks[8], (HID, d)), 'e1_w2': w(ks[9], (HID, d)), 'e1_down': w(ks[10], (d, HID)), 'e2_l1': w(ks[11], (MID, d)), 'e2_l2': w(ks[12], (HID, MID)), 'e2_l3': w(ks[13], (MID, HID)), 'e2_l4': w(ks[14], (d, MID)), 'e3_down': w(ks[15], (d, d)), 'e3_up': w(ks[16], (HID, d)), 'e3_out': w(ks[17], (d, HID))}
    _L0_ffn_in = _L0_ffn_setup()
    _d = {'L0_attn_z': _L0_attn_in['z'], 'L0_attn_ln_scale': _L0_attn_in['ln_scale'], 'L0_attn_ln_bias': _L0_attn_in['ln_bias'], 'L0_attn_w_qkv': _L0_attn_in['w_qkv'], 'L0_attn_w_proj': _L0_attn_in['w_proj'], 'L0_attn_b_proj': _L0_attn_in['b_proj'], 'L0_ffn_n1_w': _L0_ffn_in['n1_w'], 'L0_ffn_n2_w': _L0_ffn_in['n2_w'], 'L0_ffn_wq': _L0_ffn_in['wq'], 'L0_ffn_wk': _L0_ffn_in['wk'], 'L0_ffn_wv': _L0_ffn_in['wv'], 'L0_ffn_wo': _L0_ffn_in['wo'], 'L0_ffn_qn_w': _L0_ffn_in['qn_w'], 'L0_ffn_kn_w': _L0_ffn_in['kn_w'], 'L0_ffn_gate_w': _L0_ffn_in['gate_w'], 'L0_ffn_e0_up': _L0_ffn_in['e0_up'], 'L0_ffn_e0_down': _L0_ffn_in['e0_down'], 'L0_ffn_e1_w1': _L0_ffn_in['e1_w1'], 'L0_ffn_e1_w2': _L0_ffn_in['e1_w2'], 'L0_ffn_e1_down': _L0_ffn_in['e1_down'], 'L0_ffn_e2_l1': _L0_ffn_in['e2_l1'], 'L0_ffn_e2_l2': _L0_ffn_in['e2_l2'], 'L0_ffn_e2_l3': _L0_ffn_in['e2_l3'], 'L0_ffn_e2_l4': _L0_ffn_in['e2_l4'], 'L0_ffn_e3_down': _L0_ffn_in['e3_down'], 'L0_ffn_e3_up': _L0_ffn_in['e3_up'], 'L0_ffn_e3_out': _L0_ffn_in['e3_out']}
    _x0 = _d['L0_attn_z']
    _d['L0_attn_z'] = jax.random.normal(jax.random.fold_in(jax.random.key(seed), 1), (8, 512, 128), dtype=_x0.dtype)
    del _x0
    return _d

def reference(L0_attn_z, L0_attn_ln_scale, L0_attn_ln_bias, L0_attn_w_qkv, L0_attn_w_proj, L0_attn_b_proj, L0_ffn_n1_w, L0_ffn_n2_w, L0_ffn_wq, L0_ffn_wk, L0_ffn_wv, L0_ffn_wo, L0_ffn_qn_w, L0_ffn_kn_w, L0_ffn_gate_w, L0_ffn_e0_up, L0_ffn_e0_down, L0_ffn_e1_w1, L0_ffn_e1_w2, L0_ffn_e1_down, L0_ffn_e2_l1, L0_ffn_e2_l2, L0_ffn_e2_l3, L0_ffn_e2_l4, L0_ffn_e3_down, L0_ffn_e3_up, L0_ffn_e3_out):

    def _L0_attn_ref(z, ln_scale, ln_bias, w_qkv, w_proj, b_proj):
        import jax, jax.numpy as jnp
        import numpy as np
        B, N, D, H = (2, 256, 128, 16)
        HD = D // H
        SCALING = (D / H) ** 0.5
        EPS = 1e-05
        b, n, d = z.shape
        mu = jnp.mean(z, axis=-1, keepdims=True)
        var = jnp.mean(jnp.square(z - mu), axis=-1, keepdims=True)
        zn = (z - mu) / jnp.sqrt(var + EPS) * ln_scale + ln_bias
        qkv = zn @ w_qkv
        qkv5 = qkv.reshape(b, n, H, HD, 3)
        q = jnp.transpose(qkv5[..., 0], (0, 2, 1, 3))
        k = jnp.transpose(qkv5[..., 1], (0, 2, 1, 3))
        v = jnp.transpose(qkv5[..., 2], (0, 2, 1, 3))
        scores = jnp.einsum('bhqd,bhkd->bhqk', q, k) / SCALING
        att = jax.nn.softmax(scores, axis=-1)
        out = jnp.einsum('bhal,bhlv->bhav', att, v)
        out = jnp.transpose(out, (0, 2, 1, 3)).reshape(b, n, d)
        out = out @ w_proj + b_proj
        return z + out

    def _L0_ffn_ref(x, n1_w, n2_w, wq, wk, wv, wo, qn_w, kn_w, gate_w, e0_up, e0_down, e1_w1, e1_w2, e1_down, e2_l1, e2_l2, e2_l3, e2_l4, e3_down, e3_up, e3_out):
        import jax, jax.numpy as jnp
        import numpy as np
        DIM = 128
        HEADS = 16
        HD = DIM // HEADS
        M = 32
        E = 4
        K = 2
        HID = 256
        MID = 256
        LB = 0.01
        EPS = 1.1920929e-07

        def _rms(x, w):
            return x * jax.lax.rsqrt(jnp.mean(x * x, axis=-1, keepdims=True) + EPS) * w

        def _gelu(x):
            return jax.nn.gelu(x, approximate=False)
        B, T, C = x.shape
        h = _rms(x, n1_w)
        heads = lambda w_: (h @ w_.T).reshape(B, T, HEADS, HD).transpose(0, 2, 1, 3)
        q = _rms(heads(wq), qn_w)
        k = _rms(heads(wk), kn_w)
        v = heads(wv)
        scores = jnp.einsum('bhqd,bhkd->bhqk', q, k) * HD ** (-0.5)
        causal = jnp.tril(jnp.ones((T, T), bool))
        scores = jnp.where(causal[None, None], scores, -jnp.inf)
        attn = jax.nn.softmax(scores, axis=-1)
        ao = jnp.einsum('bhqk,bhkd->bhqd', attn, v).transpose(0, 2, 1, 3).reshape(B, T, C) @ wo.T
        ao = ao.at[:, :, :M].set(0.0)
        x = x + ao
        xf = _rms(x, n2_w).reshape(-1, C)
        N = xf.shape[0]
        logits = jnp.nan_to_num(xf @ gate_w.T)
        probs = jax.nn.softmax(logits, axis=-1)
        topv, topi = jax.lax.top_k(probs, K)
        topv = topv / (topv.sum(-1, keepdims=True) + 1e-08)
        wts = jnp.zeros((N, E), x.dtype).at[jnp.arange(N)[:, None], topi].add(topv)
        o0 = _gelu(xf @ e0_up.T) @ e0_down.T
        o1 = jax.nn.silu(xf @ e1_w1.T) * (xf @ e1_w2.T) @ e1_down.T
        o2 = _gelu(_gelu(_gelu(xf @ e2_l1.T) @ e2_l2.T) @ e2_l3.T) @ e2_l4.T
        o3 = _gelu(_gelu(xf @ e3_down.T) @ e3_up.T) @ e3_out.T
        moe = wts[:, 0:1] * o0 + wts[:, 1:2] * o1 + wts[:, 2:3] * o2 + wts[:, 3:4] * o3
        moe = moe.reshape(B, T, C).at[:, :, :M].set(0.0)
        return x + moe
    x = L0_attn_z
    x = x + _L0_attn_ref(_layernorm(x, axis=-1), L0_attn_ln_scale, L0_attn_ln_bias, L0_attn_w_qkv, L0_attn_w_proj, L0_attn_b_proj)
    x = x + _L0_ffn_ref(_layernorm(x, axis=-1), L0_ffn_n1_w, L0_ffn_n2_w, L0_ffn_wq, L0_ffn_wk, L0_ffn_wv, L0_ffn_wo, L0_ffn_qn_w, L0_ffn_kn_w, L0_ffn_gate_w, L0_ffn_e0_up, L0_ffn_e0_down, L0_ffn_e1_w1, L0_ffn_e1_w2, L0_ffn_e1_down, L0_ffn_e2_l1, L0_ffn_e2_l2, L0_ffn_e2_l3, L0_ffn_e2_l4, L0_ffn_e3_down, L0_ffn_e3_up, L0_ffn_e3_out)
    return x

_drawn_inputs = setup_inputs


def setup_inputs(seed=0):
    import zlib

    import numpy as np

    out = dict(_drawn_inputs(seed))
    spreads = {'L0_attn_ln_scale': (1.0, 0.6),
     'L0_attn_ln_bias': (0.0, 0.1),
     'L0_attn_b_proj': (0.0, 0.1),
     'L0_ffn_n1_w': (1.0, 0.6),
     'L0_ffn_n2_w': (1.0, 0.6),
     'L0_ffn_qn_w': (1.0, 0.6),
     'L0_ffn_kn_w': (1.0, 0.6)}
    factors = {'L0_ffn_wq': 8.0,
     'L0_ffn_wk': 8.0,
     'L0_ffn_wv': 8.0,
     'L0_ffn_wo': 8.0,
     'L0_ffn_gate_w': 8.0,
     'L0_ffn_e0_up': 8.0,
     'L0_ffn_e0_down': 8.0,
     'L0_ffn_e1_w1': 8.0,
     'L0_ffn_e1_w2': 8.0,
     'L0_ffn_e1_down': 8.0,
     'L0_ffn_e2_l1': 8.0,
     'L0_ffn_e2_l2': 8.0,
     'L0_ffn_e2_l3': 8.0,
     'L0_ffn_e2_l4': 8.0,
     'L0_ffn_e3_down': 8.0,
     'L0_ffn_e3_up': 8.0,
     'L0_ffn_e3_out': 8.0}
    for name, (base, spread) in spreads.items():
        noise = np.random.default_rng([zlib.crc32(name.encode()), seed]).standard_normal(out[name].shape)
        drawn = base * np.exp(spread * noise) if base else spread * noise
        out[name] = jnp.asarray(drawn.astype(out[name].dtype))
    for name, factor in factors.items():
        out[name] = (out[name] * factor).astype(out[name].dtype)
    return out
```

```python
from contextlib import ExitStack

import numpy as np
import concourse.bass as bass
from concourse import mybir

ALU = mybir.AluOpType
ACT = mybir.ActivationFunctionType
F32 = mybir.dt.float32
BF16 = mybir.dt.bfloat16
U32 = mybir.dt.uint32
AX = mybir.AxisListType

P = 128
SEQS, TOKENS, D = 8, 512, 128
HEADS, HD = 16, 8
BLOCKS = TOKENS // P
GROUP = 4
GROUPS = HEADS // GROUP
ROWS = 64
PAIRS = HEADS // 2
PARTS = 6
MAX_ROW = PARTS * HD
KEPT = 32
OUTC = D - KEPT
EXPERTS = 4
STEPS = GROUPS * BLOCKS
TILES = HEADS * BLOCKS
SCALE = float(HD) ** -0.5
LN_EPS = 1e-5
RMS_EPS = 1.1920929e-07
MASKED = -1e30
F32_MAX = 3.4028234663852886e38

WQKV2, WO, E0_UP, E1_W1, E1_W2, E2_L1, E3_DOWN, E2_L2, E2_L3, E3_UP, E0_DN, E1_DN, E2_DN, E3_DN = (
    0, 3, 4, 6, 8, 10, 12, 13, 17, 21, 23, 25, 27, 29)
NWT = 31

W_LAYER = 2 + 4 + 2 * STEPS
W_FFN = 8
W_SEQ = 2 * W_LAYER + W_FFN
W_SETUP = (NWT + 7) // 8
S_LAYER = TILES + 1
S_SEQ = 2 * S_LAYER + BLOCKS
T_LAYER = 2 + 2 * GROUPS
T_SEQ = 2 * T_LAYER + 2
T_READ = 2 * GROUPS + 1


def turn_queries(g):
    return 1 if g == 0 else 2 * g


def turn_output(g):
    return 2 * g + 3 if g < GROUPS - 1 else 2 * GROUPS


TURN_ATT = 2 * GROUPS + 1


def program(nc, t, out):
    with ExitStack() as ctx:
        def sb(name, shape, dt=F32):
            return ctx.enter_context(nc.sbuf_tensor(name, shape, dt))

        def psum(name, shape, dt=F32):
            return ctx.enter_context(nc.psum_tensor(name, shape, dt))

        def sem(name):
            return ctx.enter_context(nc.semaphore(name))

        stage = sb("stage", [P, NWT, P])
        wt = sb("wt", [P, NWT, P])
        wqkv_raw = sb("wqkv_raw", [P, 3 * D])
        wqkv1 = sb("wqkv1", [P, 3, D])
        wproj = sb("wproj", [P, D])
        gate_raw = sb("gate_raw", [EXPERTS, D])
        gate_t = sb("gate_t", [P, EXPERTS])
        row = sb("row", [1, D + 2 * HD])
        ones_row = sb("ones_row", [1, P])
        b_proj = sb("b_proj", [P, D])
        qk_w = sb("qk_w", [P, 2, HD])
        cols = sb("cols", [P, 4])
        id_f = sb("id_f", [P, P])
        id_b = sb("id_b", [P, P], BF16)
        mask_f = sb("mask_f", [P, 2, P])
        mask_qk = sb("mask_qk", [P, P], BF16)
        mask_kq = sb("mask_kq", [P, P], BF16)
        before = sb("before", [P, EXPERTS, EXPERTS])
        behind = sb("behind", [P, EXPERTS, EXPERTS])
        credit = sb("credit", [P, 2])

        x = sb("x", [P, BLOCKS, D])
        z = sb("z", [P, BLOCKS, D])
        n = sb("n", [P, BLOCKS, D])
        x1 = sb("x1", [P, BLOCKS, D])
        y = sb("y", [P, BLOCKS, D])
        res = sb("res", [P, BLOCKS, D])
        bn = sb("bn", [P, BLOCKS, 6])
        mv = sb("mv", [P, BLOCKS, 2])
        ms = sb("ms", [P, BLOCKS])
        ms2 = sb("ms2", [P, BLOCKS])
        eps = sb("eps", [P, 3, BLOCKS])
        rstd = sb("rstd", [P, BLOCKS])
        n_t = sb("n_t", [P, TOKENS])
        qk = sb("qk", [P, 2, BLOCKS, D])
        sq = sb("sq", [P, 2, BLOCKS, D])
        hsum = sb("hsum", [P, 2 * BLOCKS * HEADS])
        hstep = sb("hstep", [P, 2 * BLOCKS * HEADS])
        hrstd = sb("hrstd", [P, 2 * BLOCKS * HEADS])
        rest = sb("rest", [P, 2, BLOCKS, D])
        part1 = sb("part1", [P, 2, BLOCKS, D], BF16)
        part2 = sb("part2", [P, 2, BLOCKS, D], BF16)
        q_tok = sb("q_tok", [P, BLOCKS, HEADS, ROWS], BF16)
        k_tok = sb("k_tok", [P, BLOCKS, HEADS, ROWS], BF16)
        k_t = sb("k_t", [P, PAIRS, TOKENS], BF16)
        q_t = sb("q_t", [P, 2, PAIRS, TOKENS], BF16)
        v_one = sb("v_one", [P, BLOCKS, HEADS, 32])
        neg_max = sb("neg_max", [P, BLOCKS, HEADS])
        probs = sb("probs", [P, 2, GROUP, TOKENS])
        o_t = sb("o_t", [P, TOKENS])
        rec = sb("rec", [P, BLOCKS, GROUP])
        att = sb("att", [P, BLOCKS, D])
        att_t = sb("att_t", [P, TOKENS])
        hid = {name: sb(name, [P, 2, TOKENS]) for name in ("h_e1", "h_l1", "h_l2", "h_l3", "h_e3", "h_e0")}
        h_e3d = sb("h_e3d", [P, TOKENS])
        lg = sb("lg", [P, BLOCKS, EXPERTS])
        lg_ok = sb("lg_ok", [P, BLOCKS, EXPERTS], U32)
        lgc = sb("lgc", [P, BLOCKS, EXPERTS])
        lmax = sb("lmax", [P, BLOCKS])
        lexp = sb("lexp", [P, BLOCKS, EXPERTS])
        prob = sb("prob", [P, BLOCKS, EXPERTS])
        ahead = sb("ahead", [P, BLOCKS, EXPERTS, EXPERTS])
        ahead2 = sb("ahead2", [P, BLOCKS, EXPERTS, EXPERTS])
        rank = sb("rank", [P, BLOCKS, EXPERTS])
        wts = sb("wts", [P, BLOCKS, EXPERTS])

        wide = [psum(f"wide{i}", [P, 2, 512]) for i in range(2)]
        score = [psum(f"score{i}", [P, 512]) for i in range(2)]
        pv = psum("pv", [P, 512])
        turn = psum("turn", [P, 512])
        turn_tok = turn[:, :].rearrange("p (t c) -> p t c", t=BLOCKS)

        w_loaded = sem("w_loaded")
        x_loaded = sem("x_loaded")
        out_stored = sem("out_stored")
        consts = sem("consts")
        w_ready = sem("w_ready")
        wide_full = sem("wide_full")
        wide_free = [sem(f"wide_free{i}") for i in range(2)]
        score_full = sem("score_full")
        score_free = sem("score_free")
        turn_full = sem("turn_full")
        turn_free = sem("turn_free")
        stats_ready = sem("stats_ready")
        rstd_ready = sem("rstd_ready")
        q_even = sem("q_even")
        q3_ready = sem("q3_ready")
        pool_step = sem("pool_step")
        z_ready = sem("z_ready")
        n_ready = sem("n_ready")
        nt_ready = sem("nt_ready")
        res_ready = sem("res_ready")
        x1_ready = sem("x1_ready")
        y_ready = sem("y_ready")
        qk_ready = sem("qk_ready")
        parts_ready = sem("parts_ready")
        qtok_ready = sem("qtok_ready")
        ktok_ready = sem("ktok_ready")
        kt_ready = sem("kt_ready")
        qt_ready = sem("qt_ready")
        max_ready = sem("max_ready")
        qmax_ready = sem("qmax_ready")
        exp_done = sem("exp_done")
        pv_done = sem("pv_done")
        ot_ready = sem("ot_ready")
        att_ready = sem("att_ready")
        att_t_ready = sem("att_t_ready")
        logits_ready = sem("logits_ready")
        lexp_ready = sem("lexp_ready")
        hid_ready = sem("hid_ready")
        gated_ready = sem("gated_ready")

        W_LOADS = 26
        block = ctx.enter_context(nc.Block())

        @block.sync
        def _(sp):
            def load(dst, src):
                sp.dma_start(dst, src).then_inc(w_loaded, 16)

            load(wqkv_raw[:, :], t["L0_attn_w_qkv"])
            for i, name in enumerate(("ln_scale", "ln_bias")):
                load(cols[:, i:i + 1], t[f"L0_attn_{name}"].rearrange("(p a) -> p a", a=1))
            for i, name in enumerate(("n1_w", "n2_w")):
                load(cols[:, 2 + i:3 + i], t[f"L0_ffn_{name}"].rearrange("(p a) -> p a", a=1))
            load(row[:, 0:D], t["L0_attn_b_proj"].rearrange("(a n) -> a n", a=1))
            load(row[:, D:D + HD], t["L0_ffn_qn_w"].rearrange("(a n) -> a n", a=1))
            load(row[:, D + HD:], t["L0_ffn_kn_w"].rearrange("(a n) -> a n", a=1))
            load(wproj[:, :], t["L0_attn_w_proj"])
            load(gate_raw[:, :], t["L0_ffn_gate_w"])
            for i, name in enumerate(("wq", "wk", "wv", "wo")):
                load(stage[:, i, :], t[f"L0_ffn_{name}"])
            load(stage[:, E3_DOWN, :], t["L0_ffn_e3_down"])
            for at, name in ((E0_UP, "e0_up"), (E1_W1, "e1_w1"), (E1_W2, "e1_w2"), (E2_L1, "e2_l1"), (E3_UP, "e3_up")):
                sp.dma_start(stage[:, at:at + 2, :], t[f"L0_ffn_{name}"].rearrange("(a p) c -> p a c", p=P)).then_inc(w_loaded, 16)
            for at, name in ((E2_L2, "e2_l2"), (E2_L3, "e2_l3")):
                sp.dma_start(stage[:, at:at + 4, :].rearrange("p (a k) c -> p a (k c)", a=2),
                             t[f"L0_ffn_{name}"].rearrange("(a p) n -> p a n", p=P)).then_inc(w_loaded, 16)
            for at, name in ((E0_DN, "e0_down"), (E1_DN, "e1_down"), (E2_DN, "e2_l4"), (E3_DN, "e3_out")):
                load(stage[:, at:at + 2, :].rearrange("p k c -> p (k c)"), t[f"L0_ffn_{name}"])
            src = t["L0_attn_z"].rearrange("b (t p) d -> b p t d", p=P)
            dst = out.rearrange("b (t p) d -> b p t d", p=P)
            sp.dma_start(x[:, :, :], src[0]).then_inc(x_loaded, 16)
            for b in range(SEQS):
                if b + 1 < SEQS:
                    sp.wait_ge(res_ready, 3 * b + 1)
                    sp.dma_start(x[:, :, :], src[b + 1]).then_inc(x_loaded, 16)
                sp.wait_ge(score_free, S_SEQ * (b + 1) + 2)
                sp.dma_start(dst[b], res[:, :, :]).then_inc(out_stored, 16)
            sp.wait_ge(out_stored, 16 * (SEQS + 1))

        @block.gpsimd
        def _(pool):
            steps = [0]

            def link(ins):
                steps[0] += 1
                ins.then_inc(pool_step, 1)
                pool.wait_ge(pool_step, steps[0])

            nc.gpsimd.memset(id_f[:, :], 0.0)
            nc.gpsimd.memset(mask_f[:, :, :], 0.0)
            nc.gpsimd.memset(before[:, :, :], 1.0)
            for i, value in enumerate((LN_EPS, RMS_EPS, -0.5)):
                nc.gpsimd.memset(eps[:, i, :], value)
            nc.gpsimd.memset(behind[:, :, :], 1.0)
            link(nc.gpsimd.memset(ones_row[:, :], 1.0))
            nc.gpsimd.affine_select(out=id_f[:, :], in_=id_f[:, :], compare_op=ALU.not_equal, fill=1.0,
                                    base=0, pattern=[[-1, P]], channel_multiplier=1)
            nc.gpsimd.affine_select(out=mask_f[:, 0, :], in_=mask_f[:, 0, :], compare_op=ALU.is_ge, fill=MASKED,
                                    base=0, pattern=[[-1, P]], channel_multiplier=1)
            nc.gpsimd.affine_select(out=mask_f[:, 1, :], in_=mask_f[:, 1, :], compare_op=ALU.is_ge, fill=MASKED,
                                    base=0, pattern=[[1, P]], channel_multiplier=-1)
            nc.gpsimd.affine_select(out=before[:, :, :], in_=before[:, :, :], compare_op=ALU.is_gt, fill=0.0,
                                    base=0, pattern=[[1, EXPERTS], [-1, EXPERTS]], channel_multiplier=0)
            link(nc.gpsimd.affine_select(out=behind[:, :, :], in_=behind[:, :, :], compare_op=ALU.is_gt, fill=0.0,
                                         base=0, pattern=[[-1, EXPERTS], [1, EXPERTS]], channel_multiplier=0))
            nc.gpsimd.tensor_copy(id_b[:, :], id_f[:, :])
            nc.gpsimd.tensor_copy(mask_qk[:, :], mask_f[:, 0, :])
            nc.gpsimd.tensor_copy(mask_kq[:, :], mask_f[:, 1, :]).then_inc(consts, 1)
            nc.gpsimd.memset(q_tok[:, :, :, :], 0.0)
            nc.gpsimd.memset(q_t[:, :, :, :], 0.0)
            nc.gpsimd.memset(v_one[:, :, :, :], 0.0)
            link(nc.gpsimd.memset(k_tok[:, :, :, :], 0.0))
            nc.gpsimd.memset(v_one[:, :, :, HD:HD + 1], 1.0)
            nc.gpsimd.memset(k_tok[:, :, :, MAX_ROW:MAX_ROW + 2], 1.0).then_inc(consts, 1)
            nc.gpsimd.memset(credit[:, 1:2], 0.0).then_inc(out_stored, 16)
            SETUP = steps[0]
            pool.wait_ge(w_ready, 3)

            with pool.Fori(0, SEQS) as b:
                def one_over_root(which, mean_square):
                    pool.wait_ge(stats_ready, b * 5 + (which + 1))
                    if mean_square:
                        nc.gpsimd.tensor_tensor(ms2[:, :], mv[:, :, 0], mv[:, :, 0], ALU.mult)
                        pool.drain()
                        nc.gpsimd.tensor_tensor(ms2[:, :], ms2[:, :], mv[:, :, 1], ALU.add)
                        pool.drain()
                        nc.gpsimd.tensor_tensor(ms[:, :], ms2[:, :], eps[:, 1, :], ALU.add)
                    else:
                        nc.gpsimd.tensor_tensor(ms[:, :], mv[:, :, 1], eps[:, 0, :], ALU.add)
                    pool.drain()
                    nc.gpsimd.tensor_tensor(rstd[:, :], ms[:, :], eps[:, 2, :], ALU.pow).then_inc(rstd_ready, 1)

                one_over_root(0, False)
                one_over_root(1, False)
                pool.wait_ge(out_stored, b * 16 + 16)
                nc.gpsimd.tensor_tensor(res[:, :, :], x[:, :, :], z[:, :, :], ALU.add)
                pool.drain()
                nc.gpsimd.tensor_tensor(res[:, :, :], res[:, :, :],
                                        b_proj[:, :].unsqueeze(1).broadcast_to([P, BLOCKS, D]), ALU.add).then_inc(res_ready, 1)
                for layer in range(2):
                    if layer == 1:
                        one_over_root(2, False)
                        one_over_root(3, True)
                    k_rows = k_tok[:, :, :, :].rearrange("p t h r -> p (t h) r")[:, :, 0:MAX_ROW].rearrange(
                        "p g (s d) -> p g s d", d=HD)
                    p1, p2, r = (a[:, 1, :, :].rearrange("p t (h d) -> p (t h) d", d=HD) for a in (part1, part2, rest))
                    G = BLOCKS * HEADS
                    pool.wait_ge(parts_ready, b * 4 + (2 * layer + 2))
                    nc.gpsimd.tensor_tensor(k_rows[:, :, 5, :], r, p2, ALU.subtract)
                    nc.gpsimd.tensor_copy(k_rows[:, :, 0:5:2, :], p1.unsqueeze(2).broadcast_to([P, G, 3, HD]))
                    nc.gpsimd.tensor_copy(k_rows[:, :, 1:4:2, :], p2.unsqueeze(2).broadcast_to([P, G, 2, HD])).then_inc(ktok_ready, 1)
                one_over_root(4, True)
                nc.gpsimd.tensor_tensor(res[:, :, :], x1[:, :, :], y[:, :, :], ALU.add).then_inc(res_ready, 2)

        @block.scalar
        def _(act):
            act.wait_ge(w_loaded, 16 * W_LOADS)
            raw = wqkv_raw[:, :].rearrange("p (n j) -> p j n", j=3)
            nc.scalar.activation(wqkv1[:, 0, :], raw[:, 0, :], ACT.Copy, scale=SCALE)
            nc.scalar.activation(wqkv1[:, 1:3, :], raw[:, 1:3, :], ACT.Copy).then_inc(w_ready, 1)
            for u in range(0, W_SETUP, 2):
                act.wait_ge(wide_full, u + 1)
                nc.scalar.activation(wt[:, 8 * u:8 * u + 8, :].rearrange("p (a c) n -> p a (c n)", a=2),
                                     wide[0][:, :, :], ACT.Copy).then_inc(wide_free[0], 1)

            with act.Fori(0, SEQS) as b:
                def wide_done(ins, u):
                    ins.then_inc(wide_free[u % 2], 1)

                for layer in range(2):
                    w0, t0 = W_LAYER * layer, T_LAYER * layer
                    act.wait_ge(turn_full, b * T_SEQ + (1 + t0 + 1))
                    if layer == 0:
                        ins = nc.scalar.activation(n_t[:, :], turn[:, :], ACT.Identity, scale=cols[:, 0:1], bias=cols[:, 1:2])
                    else:
                        ins = nc.scalar.activation(n_t[:, :], turn[:, :], ACT.Copy, scale=cols[:, 2:3])
                    ins.then_inc(nt_ready, 1)
                    for u in range(2):
                        act.wait_ge(wide_full, b * W_SEQ + (W_SETUP + w0 + u + 1))
                        nc.scalar.activation(qk[:, :, 2 * u:2 * u + 2, :],
                                             wide[u][:, :, 0:2 * D].rearrange("p t (a n) -> p a t n", a=2), ACT.Copy).then_inc(qk_ready, 1)
                        for k in range(2):
                            ins = nc.scalar.activation(
                                v_one[:, 2 * u + k, :, 0:HD],
                                wide[u][:, k, 2 * D:3 * D].rearrange("p (h d) -> p h d", d=HD), ACT.Copy)
                        wide_done(ins, u)
                    q_rows = q_tok[:, :, :, :].rearrange("p t h r -> p (t h) r")[:, :, 0:MAX_ROW].rearrange(
                        "p g (s d) -> p g s d", d=HD)
                    p1, p2 = (a[:, 0, :, :].rearrange("p t (h d) -> p (t h) d", d=HD) for a in (part1, part2))
                    G = BLOCKS * HEADS
                    act.wait_ge(parts_ready, b * 4 + (2 * layer + 1))
                    nc.scalar.activation(q_rows[:, :, 0:2, :], p1.unsqueeze(2).broadcast_to([P, G, 2, HD]), ACT.Copy)
                    nc.scalar.activation(q_rows[:, :, 5, :], p1, ACT.Copy)
                    act.wait_ge(parts_ready, b * 4 + (2 * layer + 2))
                    nc.scalar.activation(q_rows[:, :, 2:4, :], p2.unsqueeze(2).broadcast_to([P, G, 2, HD]), ACT.Copy).then_inc(qtok_ready, 1)
                    for half in range(2):
                        u = 2 + 2 * half
                        act.wait_ge(wide_full, b * W_SEQ + (W_SETUP + w0 + u + 1))
                        ins = nc.scalar.activation(k_t[:, 4 * half:4 * half + 4, :].rearrange("p a n -> p (a n)"),
                                                   wide[0][:, :, :].rearrange("p a n -> p (a n)").bitcast(BF16), ACT.Copy)
                        ins.then_inc(wide_free[0], 1)
                        act.wait_ge(wide_full, b * W_SEQ + (W_SETUP + w0 + u + 2))
                        nc.scalar.activation(q_t[0:ROWS, 0, 4 * half:4 * half + 4, :].rearrange("p a n -> p (a n)"),
                                             wide[1][0:ROWS, :, :].rearrange("p a n -> p (a n)").bitcast(BF16), ACT.Copy).then_inc(q_even, 1)

                    for i in range(STEPS):
                        g, kb = divmod(i, BLOCKS)
                        if kb == 0:
                            act.wait_ge(turn_full, b * T_SEQ + (1 + t0 + turn_queries(g) + 1))
                            for k in range(2):
                                ins = nc.scalar.activation(
                                    q_t[ROWS * k:ROWS * (k + 1), k, 2 * g:2 * g + 2, :].rearrange("p a n -> p (a n)"),
                                    turn[ROWS * k:ROWS * (k + 1), :].bitcast(BF16), ACT.Copy)
                            ins.then_inc(qmax_ready, 1)
                        if i >= 2:
                            act.wait_ge(pv_done, b * 2 * STEPS + (STEPS * layer + i - 1))
                        c0 = P * kb if layer else 0
                        for half in range(2):
                            u = 6 + 2 * i + half
                            act.wait_ge(wide_full, b * W_SEQ + (W_SETUP + w0 + u + 1))
                            nc.scalar.activation(probs[:, i % 2, 2 * half:2 * half + 2, c0:], wide[u % 2][:, :, c0:],
                                                 ACT.Exp).then_inc(wide_free[u % 2], 1)
                        if kb == 0 and g > 0:
                            act.wait_ge(pv_done, b * 2 * STEPS + (STEPS * layer + i))
                            nc.scalar.activation(o_t[:, :], pv[:, :], ACT.Copy).then_inc(ot_ready, 1)
                    act.wait_ge(pv_done, b * 2 * STEPS + (STEPS * layer + STEPS))
                    nc.scalar.activation(o_t[:, :], pv[:, :], ACT.Copy).then_inc(ot_ready, 1)
                    act.wait_ge(turn_full, b * T_SEQ + (1 + t0 + TURN_ATT + 1))
                    nc.scalar.activation(att_t[:, :], turn[:, :], ACT.Copy).then_inc(att_t_ready, 1)

                act.wait_ge(turn_full, b * T_SEQ + (1 + 2 * T_LAYER + 1))
                nc.scalar.activation(n_t[:, :], turn[:, :], ACT.Copy, scale=cols[:, 3:4]).then_inc(nt_ready, 1)
                act.wait_ge(logits_ready, b + 1)
                nc.scalar.activation(lexp[:, :, :], lgc[:, :, :], ACT.Exp).then_inc(lexp_ready, 1)
                w0 = 2 * W_LAYER
                for u, (name, fn) in enumerate((("h_e1", ACT.Silu), ("gate of expert 1, VectorE's", None), ("h_l1", ACT.Gelu),
                                                ("h_e3d", ACT.Gelu), ("h_l2", ACT.Gelu), ("h_e3", ACT.Gelu),
                                                ("h_l3", ACT.Gelu), ("h_e0", ACT.Gelu))):
                    if fn is None:
                        continue
                    act.wait_ge(wide_full, b * W_SEQ + (W_SETUP + w0 + u + 1))
                    if name == "h_e3d":
                        ins = nc.scalar.activation(h_e3d[:, :], wide[u % 2][:, 0, :], fn)
                    else:
                        ins = nc.scalar.activation(hid[name][:, :, :], wide[u % 2][:, :, :], fn)
                    ins.then_inc(wide_free[u % 2], 1)

        @block.vector
        def _(dve):
            nc.vector.memset(credit[:, 0:1], 0.0).then_inc(score_free, 2)
            for u in range(1, W_SETUP, 2):
                dve.wait_ge(wide_full, u + 1)
                m = min(8, NWT - 8 * u)
                nc.vector.tensor_copy(wt[:, 8 * u:8 * u + m, :].rearrange("p a n -> p (a n)"),
                                      wide[1][:, :, :].rearrange("p a n -> p (a n)")[:, 0:m * P]).then_inc(wide_free[1], 1)
            dve.wait_ge(turn_full, 1)
            nc.vector.tensor_copy(gate_t[:, :], turn[:, 0:EXPERTS])
            nc.vector.tensor_copy(b_proj[:, :], turn[:, 128:256]).then_inc(w_ready, 1)
            rows = turn[:, 256:256 + 2 * HD].rearrange("p (a d) -> p a d", a=2)
            nc.vector.tensor_copy(qk_w[:, 1, :], rows[:, 1, :])
            nc.vector.tensor_scalar(qk_w[:, 0, :], rows[:, 0, :], SCALE, None, ALU.mult).then_inc(turn_free, 1)
            nc.vector.memset(lgc[:, :, :], 0.0).then_inc(w_ready, 1)

            with dve.Fori(0, SEQS) as b:
                def settle():
                    dve.drain()

                def stats(src, which):
                    for k in range(BLOCKS):
                        ins = nc.vector.bn_stats(bn[:, k, :], src[:, k, :])
                    settle()
                    for k in range(BLOCKS):
                        ins = nc.vector.bn_aggr(mv[:, k, :], bn[:, k, :])
                    ins.then_inc(stats_ready, 1)
                    dve.wait_ge(rstd_ready, b * 5 + (which + 1))

                def layernorm(dst, src, which):
                    stats(src, which)
                    for k in range(BLOCKS):
                        ins = nc.vector.tensor_scalar(dst[:, k, :], src[:, k, :], mv[:, k, 0:1], rstd[:, k:k + 1],
                                                      ALU.subtract, ALU.mult)
                    return ins

                def rms(dst, src, which):
                    stats(src, which)
                    for k in range(BLOCKS):
                        ins = nc.vector.tensor_scalar(dst[:, k, :], src[:, k, :], rstd[:, k:k + 1], None, ALU.mult)
                    return ins

                def normalise_output(layer, g):
                    dve.wait_ge(turn_full, b * T_SEQ + (1 + T_LAYER * layer + turn_output(g) + 1))
                    o = turn[:, :].rearrange("p (t j r) -> p t j r", t=BLOCKS, j=GROUP)
                    nc.vector.reciprocal(rec[:, :, :], o[:, :, :, HD])
                    settle()
                    ins = nc.vector.tensor_tensor(
                        att[:, :, GROUP * HD * g:GROUP * HD * (g + 1)].rearrange("p t (j d) -> p t j d", d=HD),
                        o[:, :, :, 0:HD], rec[:, :, :].unsqueeze(3).broadcast_to([P, BLOCKS, GROUP, HD]), ALU.mult)
                    ins.then_inc(turn_free, 1)

                for layer in range(2):
                    w0, s0 = W_LAYER * layer, S_LAYER * layer
                    if layer == 0:
                        dve.wait_ge(x_loaded, b * 16 + 16)
                        layernorm(z, x, 0).then_inc(z_ready, 1)
                        dve.wait_ge(z_ready, b + 1)
                        layernorm(n, z, 1).then_inc(n_ready, 1)
                    else:
                        layernorm(y, x1, 2).then_inc(y_ready, 1)
                        dve.wait_ge(y_ready, b + 1)
                        rms(n, y, 3).then_inc(n_ready, 1)
                    dve.wait_ge(qk_ready, b * 4 + (2 * layer + 2))
                    flat = qk[:, :, :, :].rearrange("p a t n -> p (a t n)")
                    if layer == 1:
                        sqf = sq[:, :, :, :].rearrange("p a t n -> p (a t n)")
                        nc.vector.tensor_tensor(sqf, flat, flat, ALU.mult)
                        settle()
                        nc.vector.tensor_reduce(hsum[:, :], sqf.rearrange("p (g d) -> p g d", d=HD), AX.X, ALU.add)
                        settle()
                        nc.vector.tensor_scalar(hsum[:, :], hsum[:, :], 1.0 / HD, RMS_EPS, ALU.mult, ALU.add)
                        settle()
                        nc.vector.tensor_scalar(hrstd[:, :].bitcast(U32), hsum[:, :].bitcast(U32), -0.5, 1597463007.0, ALU.mult, ALU.add)
                        settle()
                        for _ in range(3):
                            nc.vector.scalar_tensor_tensor(out=hstep[:, :], in0=hsum[:, :], scalar=-0.5, in1=hrstd[:, :],
                                                           op0=ALU.mult, op1=ALU.mult)
                            settle()
                            nc.vector.tensor_tensor(hstep[:, :], hstep[:, :], hrstd[:, :], ALU.mult)
                            settle()
                            nc.vector.scalar_tensor_tensor(out=hrstd[:, :], in0=hstep[:, :], scalar=1.5, in1=hrstd[:, :],
                                                           op0=ALU.add, op1=ALU.mult)
                            settle()
                        heads = flat.rearrange("p (g d) -> p g d", d=HD)
                        nc.vector.tensor_tensor(heads, heads, hrstd[:, :].unsqueeze(2).broadcast_to([P, 2 * BLOCKS * HEADS, HD]), ALU.mult)
                        settle()
                        both = flat.rearrange("p (a g d) -> p a g d", a=2, d=HD)
                        nc.vector.tensor_tensor(both, both, qk_w[:, :, :].unsqueeze(2).broadcast_to([P, 2, BLOCKS * HEADS, HD]), ALU.mult)
                        settle()
                    f1, f2, r = (a[:, :, :, :].rearrange("p a t n -> p (a t n)") for a in (part1, part2, rest))
                    nc.vector.tensor_copy(f1, flat).then_inc(parts_ready, 1)
                    settle()
                    nc.vector.tensor_tensor(r, flat, f1, ALU.subtract)
                    settle()
                    nc.vector.tensor_copy(f2, r).then_inc(parts_ready, 1)
                    settle()
                    nc.vector.memset(q_tok[:, :, :, MAX_ROW:MAX_ROW + 2], 0.0)
                    nc.vector.tensor_tensor(q_tok[:, :, :, 4 * HD:5 * HD], rest[:, 0, :, :].rearrange("p t (h d) -> p t h d", d=HD),
                                            part2[:, 0, :, :].rearrange("p t (h d) -> p t h d", d=HD), ALU.subtract).then_inc(q3_ready, 1)
                    for half in range(2):
                        u = 3 + 2 * half
                        dve.wait_ge(wide_full, b * W_SEQ + (W_SETUP + w0 + u + 1))
                        ins = nc.vector.tensor_copy(q_t[ROWS:, 1, 4 * half:4 * half + 4, :].rearrange("p a n -> p (a n)"),
                                                    wide[1][ROWS:, :, :].rearrange("p a n -> p (a n)").bitcast(BF16))
                        ins.then_inc(wide_free[1], 1)

                    for tile in range(TILES):
                        h, qb = divmod(tile, BLOCKS)
                        g = h // GROUP
                        width = P * (qb + 1) if layer else TOKENS
                        s = s0 + tile
                        dve.wait_ge(score_full, b * S_SEQ + (s + 1))
                        nc.vector.tensor_reduce(neg_max[:, qb, h:h + 1], score[s % 2][:, 0:width], AX.X, ALU.max,
                                                negate=True).then_inc(score_free, 1)
                        if tile % (TILES // GROUPS) == TILES // GROUPS - 1:
                            dve.wait_ge(score_free, b * S_SEQ + (2 + s + 1))
                            hs = slice(GROUP * g, GROUP * (g + 1))
                            nc.vector.tensor_copy(q_tok[:, :, hs, MAX_ROW], neg_max[:, :, hs])
                            settle()
                            nc.vector.tensor_tensor(q_tok[:, :, hs, MAX_ROW + 1], neg_max[:, :, hs], q_tok[:, :, hs, MAX_ROW],
                                                    ALU.subtract).then_inc(max_ready, 1)
                        if tile % (TILES // GROUPS) == 11 and g >= 2:
                            normalise_output(layer, g - 2)
                    normalise_output(layer, 2)
                    normalise_output(layer, 3)
                    s = s0 + TILES
                    dve.wait_ge(score_full, b * S_SEQ + (s + 1))
                    if layer == 0:
                        dve.wait_ge(res_ready, b * 3 + 1)
                        nc.vector.tensor_tensor(x1[:, :, :], score[s % 2][:, :].rearrange("p (t n) -> p t n", t=BLOCKS),
                                                res[:, :, :], ALU.add).then_inc(score_free, 1)
                        dve.wait_ge(score_free, b * S_SEQ + (2 + s + 1))
                    else:
                        nc.vector.tensor_tensor(y[:, :, KEPT:], score[s % 2][:, 0:BLOCKS * OUTC].rearrange("p (t n) -> p t n", t=BLOCKS),
                                                y[:, :, KEPT:], ALU.add).then_inc(score_free, 1)
                        dve.wait_ge(score_free, b * S_SEQ + (2 + s + 1))

                rms(n, y, 4).then_inc(n_ready, 1)

                dve.wait_ge(turn_full, b * T_SEQ + (1 + 2 * T_LAYER + 2))
                nc.vector.tensor_copy(lg[:, :, :], turn[:, 0:BLOCKS * EXPERTS].rearrange("p (t e) -> p t e", e=EXPERTS))
                settle()
                nc.vector.memset(lgc[:, :, :], 0.0).then_inc(turn_free, 1)
                nc.vector.tensor_tensor(lg_ok[:, :, :], lg[:, :, :], lg[:, :, :], ALU.is_equal)
                settle()
                nc.vector.copy_predicated(lgc[:, :, :], lg_ok[:, :, :], lg[:, :, :])
                settle()
                nc.vector.tensor_scalar(lg[:, :, :], lgc[:, :, :], -F32_MAX, F32_MAX, ALU.max, ALU.min)
                settle()
                nc.vector.tensor_reduce(lmax[:, :], lg[:, :, :], AX.X, ALU.max)
                settle()
                nc.vector.tensor_tensor(lgc[:, :, :], lg[:, :, :], lmax[:, :].unsqueeze(2).broadcast_to([P, BLOCKS, EXPERTS]),
                                        ALU.subtract).then_inc(logits_ready, 1)
                dve.wait_ge(lexp_ready, b + 1)
                four = [P, BLOCKS, EXPERTS, EXPERTS]
                nc.vector.tensor_reduce(lmax[:, :], lexp[:, :, :], AX.X, ALU.add)
                settle()
                nc.vector.reciprocal(lmax[:, :], lmax[:, :])
                settle()
                nc.vector.tensor_tensor(prob[:, :, :], lexp[:, :, :], lmax[:, :].unsqueeze(2).broadcast_to([P, BLOCKS, EXPERTS]), ALU.mult)
                settle()
                p_i = prob[:, :, :].unsqueeze(2).broadcast_to(four)
                p_j = prob[:, :, :].unsqueeze(3).broadcast_to(four)
                nc.vector.tensor_tensor(ahead[:, :, :, :], p_i, p_j, ALU.is_ge)
                nc.vector.tensor_tensor(ahead2[:, :, :, :], p_i, p_j, ALU.is_gt)
                settle()
                nc.vector.tensor_tensor(ahead[:, :, :, :], ahead[:, :, :, :], before[:, :, :].unsqueeze(1).broadcast_to(four), ALU.mult)
                nc.vector.tensor_tensor(ahead2[:, :, :, :], ahead2[:, :, :, :], behind[:, :, :].unsqueeze(1).broadcast_to(four), ALU.mult)
                settle()
                nc.vector.tensor_tensor(ahead[:, :, :, :], ahead[:, :, :, :], ahead2[:, :, :, :], ALU.add)
                settle()
                nc.vector.tensor_reduce(rank[:, :, :], ahead[:, :, :, :], AX.X, ALU.add)
                settle()
                nc.vector.scalar_tensor_tensor(out=wts[:, :, :], in0=rank[:, :, :], scalar=1.5, in1=prob[:, :, :],
                                                    op0=ALU.is_lt, op1=ALU.mult)
                settle()
                nc.vector.tensor_reduce(lmax[:, :], wts[:, :, :], AX.X, ALU.add)
                settle()
                nc.vector.tensor_scalar(lmax[:, :], lmax[:, :], 1e-8, None, ALU.add)
                settle()
                nc.vector.reciprocal(lmax[:, :], lmax[:, :])
                settle()
                nc.vector.tensor_tensor(wts[:, :, :], wts[:, :, :], lmax[:, :].unsqueeze(2).broadcast_to([P, BLOCKS, EXPERTS]), ALU.mult)
                settle()

                w0 = 2 * W_LAYER
                dve.wait_ge(wide_full, b * W_SEQ + (W_SETUP + w0 + 2))
                dve.wait_ge(wide_free[0], b * (W_SEQ // 2) + (W_SETUP // 2 + w0 // 2 + 1))
                nc.vector.tensor_tensor(hid["h_e1"][:, :, :], hid["h_e1"][:, :, :], wide[1][:, :, :], ALU.mult).then_inc(wide_free[1], 1)

                dve.wait_ge(res_ready, b * 3 + 3)
                for k in range(BLOCKS):
                    s = 2 * S_LAYER + k
                    dve.wait_ge(score_full, b * S_SEQ + (s + 1))
                    for e in range(EXPERTS):
                        ins = nc.vector.scalar_tensor_tensor(
                            out=res[:, k, KEPT:], in0=score[s % 2][:, OUTC * e:OUTC * (e + 1)], scalar=wts[:, k, e:e + 1],
                            in1=res[:, k, KEPT:], op0=ALU.mult, op1=ALU.add)
                        if e < EXPERTS - 1:
                            settle()
                    ins.then_inc(score_free, 1)

        @block.tensor
        def _(pe):
            pe.wait_ge(w_loaded, 16 * W_LOADS)
            pe.wait_ge(consts, 1)
            for u in range(W_SETUP):
                if u >= 2:
                    pe.wait_ge(wide_free[u % 2], u // 2)
                for k in range(8 * u, min(8 * u + 8, NWT)):
                    ins = nc.tensor.transpose(wide[u % 2][:, k % 8 // 4, k % 4 * P:k % 4 * P + P], stage[:, k, :], id_f[:, :])
                ins.then_inc(wide_full, 1)
            nc.tensor.transpose(turn[:, 0:EXPERTS], gate_raw[:, :], id_f[0:EXPERTS, 0:EXPERTS])
            nc.tensor.matmul(turn[:, 128:128 + D + 2 * HD], ones_row[:, :], row[:, :], start=True, stop=True).then_inc(turn_full, 1)
            pe.wait_ge(w_ready, 3)
            pe.wait_ge(consts, 2)

            with pe.Fori(0, SEQS) as b:
                def wide_wait(u):
                    pe.wait_ge(wide_free[u % 2], b * (W_SEQ // 2) + (W_SETUP // 2 + u // 2))

                def score_wait(s):
                    pe.wait_ge(score_free, b * S_SEQ + (2 + s - 1))

                def turn_wait(k):
                    pe.wait_ge(turn_free, b * T_READ + (1 + k))

                def turn_tokens(src):
                    for k in range(BLOCKS):
                        ins = nc.tensor.transpose(turn[:, P * k:P * (k + 1)], src[:, k, :], id_f[:, :])
                    ins.then_inc(turn_full, 1)

                for layer in range(2):
                    w0, s0, t0 = W_LAYER * layer, S_LAYER * layer, T_LAYER * layer
                    pe.wait_ge(n_ready, b * 3 + (layer + 1))
                    turn_wait(GROUPS * layer)
                    turn_tokens(n)
                    pe.wait_ge(nt_ready, b * 3 + (layer + 1))
                    w_in = wqkv1[:, :, :] if layer == 0 else wt[:, WQKV2:WQKV2 + 3, :]
                    for u in range(2):
                        wide_wait(w0 + u)
                        for k in range(2):
                            kb = 2 * u + k
                            ins = nc.tensor.matmul(wide[u][:, k, 0:3 * D], n_t[:, P * kb:P * (kb + 1)],
                                                   w_in.rearrange("p a n -> p (a n)"), start=True, stop=True)
                        ins.then_inc(wide_full, 1)
                    for u in range(2, 6):
                        src, ready = (k_tok, ktok_ready) if u % 2 == 0 else (q_tok, qtok_ready)
                        pe.wait_ge(ready, b * 2 + (layer + 1))
                        if src is q_tok:
                            pe.wait_ge(q3_ready, b * 2 + (layer + 1))
                        wide_wait(w0 + u)
                        if u == 5:
                            pe.wait_ge(q_even, b * 4 + (2 * layer + 1))
                        dst = wide[u % 2][:, :, :].rearrange("p a n -> p (a n)").bitcast(BF16)
                        for a in range(4):
                            pair = 4 * (u // 2 - 1) + a
                            for k in range(BLOCKS):
                                ins = nc.tensor.transpose(
                                    dst[:, TOKENS * a + P * k:TOKENS * a + P * (k + 1)],
                                    src[:, k, 2 * pair:2 * pair + 2, :].rearrange("p h r -> p (h r)"), id_b[:, :])
                        ins.then_inc(wide_full, 1)

                    def score_tile(tile):
                        h, qb = divmod(tile, BLOCKS)
                        s = s0 + tile
                        width = P * (qb + 1) if layer else TOKENS
                        score_wait(s)
                        if tile % (TILES // 2) == 0:
                            done_u = 3 + 2 * (tile // (TILES // 2))
                            pe.wait_ge(wide_free[0], b * (W_SEQ // 2) + (W_SETUP // 2 + (w0 + done_u - 1) // 2 + 1))
                            pe.wait_ge(wide_free[1], b * (W_SEQ // 2) + (W_SETUP // 2 + (w0 + done_u) // 2 + 1))
                            pe.wait_ge(q_even, b * 4 + (2 * layer + tile // (TILES // 2) + 1))
                        ins = nc.tensor.matmul(score[s % 2][:, 0:width], q_t[:, h % 2, h // 2, P * qb:P * (qb + 1)],
                                               k_t[:, h // 2, 0:width], start=True, stop=not layer)
                        if layer:
                            ins = nc.tensor.matmul(score[s % 2][:, P * qb:width], id_b[:, :], mask_qk[:, :], start=False, stop=True)
                        ins.then_inc(score_full, 1)

                    def shifted_scores(i, half):
                        g, kb = divmod(i, BLOCKS)
                        u = w0 + 6 + 2 * i + half
                        pair = 2 * g + half
                        c0 = P * kb if layer else 0
                        wide_wait(u)
                        for k in range(2):
                            ins = nc.tensor.matmul(wide[u % 2][:, k, c0:], k_t[:, pair, P * kb:P * (kb + 1)],
                                                   q_t[:, k, pair, c0:], start=True, stop=not layer)
                            if layer:
                                ins = nc.tensor.matmul(wide[u % 2][:, k, c0:c0 + P], id_b[:, :], mask_kq[:, :], start=False, stop=True)
                        ins.then_inc(wide_full, 1)

                    def values(i):
                        g, kb = divmod(i, BLOCKS)
                        c0 = P * kb if layer else 0
                        u = w0 + 6 + 2 * i
                        pe.wait_ge(wide_free[0], b * (W_SEQ // 2) + (W_SETUP // 2 + u // 2 + 1))
                        pe.wait_ge(wide_free[1], b * (W_SEQ // 2) + (W_SETUP // 2 + u // 2 + 1))
                        if kb == 0 and g > 0:
                            pe.wait_ge(ot_ready, b * 2 * GROUPS + (GROUPS * layer + g))
                        for j in range(GROUP):
                            ins = nc.tensor.matmul(pv[32 * j:32 * j + 32, c0:], v_one[:, kb, GROUP * g + j, :], probs[:, i % 2, j, c0:],
                                                   start=(kb == 0), stop=(kb == BLOCKS - 1), tile_position=(0, 32 * j))
                        ins.then_inc(pv_done, 1)

                    def turn_group_output(g):
                        pe.wait_ge(ot_ready, b * 2 * GROUPS + (GROUPS * layer + g + 1))
                        turn_wait(GROUPS * layer + g)
                        for k in range(BLOCKS):
                            ins = nc.tensor.transpose(turn[:, P * k:P * (k + 1)], o_t[:, P * k:P * (k + 1)], id_f[:, :])
                        ins.then_inc(turn_full, 1)

                    ahead_tiles = TILES // GROUPS + 4
                    for tile in range(ahead_tiles):
                        score_tile(tile)
                    for i in range(STEPS):
                        g, kb = divmod(i, BLOCKS)
                        if kb == 0:
                            if g == 0:
                                pe.wait_ge(q_even, b * 4 + (2 * layer + 2))
                            pe.wait_ge(max_ready, b * 2 * GROUPS + (GROUPS * layer + g + 1))
                            turn_wait(GROUPS * layer + max(0, g - 1))
                            dst = turn[:, :].bitcast(BF16)
                            for a in range(2):
                                for k in range(BLOCKS):
                                    ins = nc.tensor.transpose(
                                        dst[:, TOKENS * a + P * k:TOKENS * a + P * (k + 1)],
                                        q_tok[:, k, 4 * g + 2 * a:4 * g + 2 * a + 2, :].rearrange("p h r -> p (h r)"), id_b[:, :])
                            ins.then_inc(turn_full, 1)
                            pe.wait_ge(qmax_ready, b * 2 * GROUPS + (GROUPS * layer + g + 1))
                        tiles = range(ahead_tiles + 4 * i, min(ahead_tiles + 4 * i + 4, TILES))
                        shifted_scores(i, 0)
                        for tile in tiles[0:2]:
                            score_tile(tile)
                        shifted_scores(i, 1)
                        for tile in tiles[2:4]:
                            score_tile(tile)
                        if kb == 1 and g > 0:
                            turn_group_output(g - 1)
                        if i > 0:
                            values(i - 1)
                    values(STEPS - 1)
                    turn_group_output(GROUPS - 1)
                    turn_wait(GROUPS * (layer + 1))
                    turn_tokens(att)
                    pe.wait_ge(att_t_ready, b * 2 + (layer + 1))
                    s = s0 + TILES
                    score_wait(s)
                    width = OUTC if layer else D
                    w_out = wt[:, WO, KEPT:] if layer else wproj[:, :]
                    for k in range(BLOCKS):
                        ins = nc.tensor.matmul(score[s % 2][:, width * k:width * (k + 1)], att_t[:, P * k:P * (k + 1)], w_out,
                                               start=True, stop=True)
                    ins.then_inc(score_full, 1)

                pe.wait_ge(n_ready, b * 3 + 3)
                turn_wait(2 * GROUPS)
                turn_tokens(n)
                pe.wait_ge(nt_ready, b * 3 + 3)
                for k in range(BLOCKS):
                    ins = nc.tensor.matmul(turn[:, EXPERTS * k:EXPERTS * (k + 1)], n_t[:, P * k:P * (k + 1)], gate_t[:, :],
                                           start=True, stop=True)
                ins.then_inc(turn_full, 1)
                w0 = 2 * W_LAYER

                def layer_in(u, at, srcs, halves=2):
                    wide_wait(w0 + u)
                    for a in range(halves):
                        for k, src in enumerate(srcs):
                            ins = nc.tensor.matmul(wide[u % 2][:, a, :], wt[:, at + len(srcs) * a + k, :], src,
                                                   start=(k == 0), stop=(k == len(srcs) - 1))
                    ins.then_inc(wide_full, 1)

                def unit_written(u):
                    pe.wait_ge(wide_free[u % 2], b * (W_SEQ // 2) + (W_SETUP // 2 + (w0 + u) // 2 + 1))

                xf = n_t[:, :]
                layer_in(0, E1_W1, [xf])
                layer_in(1, E1_W2, [xf])
                layer_in(2, E2_L1, [xf])
                layer_in(3, E3_DOWN, [xf], 1)
                unit_written(2)
                layer_in(4, E2_L2, [hid["h_l1"][:, k, :] for k in range(2)])
                unit_written(3)
                layer_in(5, E3_UP, [h_e3d[:, :]])
                unit_written(4)
                layer_in(6, E2_L3, [hid["h_l2"][:, k, :] for k in range(2)])
                layer_in(7, E0_UP, [xf])
                unit_written(6)
                unit_written(7)
                for k in range(BLOCKS):
                    s = 2 * S_LAYER + k
                    score_wait(s)
                    for e, (at, name) in enumerate(((E0_DN, "h_e0"), (E1_DN, "h_e1"), (E2_DN, "h_l3"), (E3_DN, "h_e3"))):
                        for a in range(2):
                            ins = nc.tensor.matmul(score[s % 2][:, OUTC * e:OUTC * (e + 1)], hid[name][:, a, P * k:P * (k + 1)],
                                                   wt[:, at + a, KEPT:], start=(a == 0), stop=(a == 1))
                    ins.then_inc(score_full, 1)


_INS = ['L0_attn_z', 'L0_attn_ln_scale', 'L0_attn_ln_bias', 'L0_attn_w_qkv', 'L0_attn_w_proj', 'L0_attn_b_proj', 'L0_ffn_n1_w',
        'L0_ffn_n2_w', 'L0_ffn_wq', 'L0_ffn_wk', 'L0_ffn_wv', 'L0_ffn_wo', 'L0_ffn_qn_w', 'L0_ffn_kn_w', 'L0_ffn_gate_w',
        'L0_ffn_e0_up', 'L0_ffn_e0_down', 'L0_ffn_e1_w1', 'L0_ffn_e1_w2', 'L0_ffn_e1_down', 'L0_ffn_e2_l1', 'L0_ffn_e2_l2',
        'L0_ffn_e2_l3', 'L0_ffn_e2_l4', 'L0_ffn_e3_down', 'L0_ffn_e3_up', 'L0_ffn_e3_out']


def kernel(**inputs):
    import numpy as _np
    import concourse.bacc as _bacc
    from concourse import mybir as _mybir
    from concourse.bass_utils import run_bass_kernel_spmd as _run

    nc = _bacc.Bacc("TRN2", target_bir_lowering=False, num_devices=1)
    arrays, args = {}, {}
    for name in _INS:
        a = _np.ascontiguousarray(inputs[name])
        arrays[f"in_{name}_dram"] = a
        args[name] = nc.dram_tensor(f"in_{name}_dram", a.shape, _mybir.dt.from_np(a.dtype), kind="ExternalInput").ap()
    result = nc.dram_tensor("out_0_dram", (SEQS, TOKENS, D), F32, kind="ExternalOutput").ap()
    program(nc, args, result)
    r = _run(nc, [arrays], core_ids=[0])
    return r.results[0]["out_0_dram"]
```

```python
from contextlib import ExitStack

import concourse.bass as bass
from concourse import mybir

ALU = mybir.AluOpType
ACT = mybir.ActivationFunctionType
F32 = mybir.dt.float32
BF16 = mybir.dt.bfloat16
U32 = mybir.dt.uint32
AX = mybir.AxisListType

P = 128
SEQS, TOKENS, D = 8, 512, 128
HEADS, HD = 16, 8
BLOCKS = TOKENS // P
GROUP = 4
GROUPS = HEADS // GROUP
ROWS = 64
PAIRS = HEADS // 2
PARTS = 6
MAX_ROW = PARTS * HD
KEPT = 32
OUTC = D - KEPT
EXPERTS = 4
STEPS = GROUPS * BLOCKS
TILES = HEADS * BLOCKS
GTILES = TILES // GROUPS
AHEAD = GTILES + 4
LAG = 2
RING = 4
SCALE = float(HD) ** -0.5
LN_EPS = 1e-5
RMS_EPS = 1.1920929e-07
MASKED = -1e30
F32_MAX = 3.4028234663852886e38

WQKV2, WO, E0_UP, E1_W1, E1_W2, E2_L1, E3_DOWN, E2_L2, E2_L3, E3_UP, E0_DN, E1_DN, E2_DN, E3_DN = (
    0, 3, 4, 6, 8, 10, 12, 13, 17, 21, 23, 25, 27, 29)
NWT = 31

SETUP_FILLS = {"wide": (NWT + 7) // 8, "score": 2, "turn": 1, "pv": 0, "ot": 0}
FILLS = {
    "wide": ("qkv", "rows", "shifted", "expert"),
    "score": ("score", "project", "down"),
    "turn": ("norm_t", "max_rows", "group_out", "att_t", "router"),
    "pv": ("values",),
}


def tasks(att1, att2, pro1, pro2):
    order = []
    tiles = [(0, n) for n in range(AHEAD, TILES)] * att1 + [(1, n) for n in range(TILES)] * att2
    late = [(0, n) for n in range(AHEAD)] * pro1

    def scores(n, of=None):
        of = tiles if of is None else of
        for _ in range(min(n, len(of))):
            order.append(("score", *of.pop(0)))

    def add(*names):
        order.extend(names)

    side1 = {
        1: [("keep_y",)],
        2: [("rows", 1, "k", 0)], 3: [("rows", 1, "q", 0)], 5: [("rows", 1, "k", 1)], 6: [("rows", 1, "q", 1)],
    } if att2 else {}
    side2 = {}

    def put(step, *names):
        side2.setdefault(step, []).extend(names)

    if att1:
        put(0, ("values", 0, STEPS - 2))
        put(1, ("values", 0, STEPS - 1))
        put(2, ("group_out", 0, GROUPS - 1))
        put(3, ("att_t", 0))
        put(4, ("project", 0))
    if pro1:
        put(1, ("stats", 0))
        put(2, ("apply", 0), ("stats", 1))
        put(4, ("apply", 1))
        put(5, ("norm_t", 0))
        put(6, ("qkv", 0, 0))
        put(7, ("qkv", 0, 1))
    if pro2:
        put(5, ("stats", 2))
        put(6, ("apply", 2), ("stats", 3))
        put(7, ("apply", 3))
        put(9, ("norm_t", 1))
    if pro1:
        put(8, ("part1", 0))
        put(9, ("part2", 0))
        put(10, ("q_rows", 0))
        put(12, ("rows", 0, "k", 0))
        put(13, ("rows", 0, "q", 0))
        put(14, ("rows", 0, "k", 1))
        put(15, ("rows", 0, "q", 1))

    def attention(layer, side):
        for i in range(STEPS):
            g, kb = divmod(i, BLOCKS)
            if kb == 0:
                add(("max_rows", layer, g))
            scores(2)
            if i >= LAG:
                add(("values", layer, i - LAG))
            scores(1)
            add(("shifted", layer, i, 0))
            scores(1)
            add(("shifted", layer, i, 1))
            if kb == LAG and g > 0:
                add(("group_out", layer, g - 1))
            add(*side.get(i, ()))

    if att1:
        attention(0, side1)
    elif att2:
        for names in side1.values():
            add(*names)
        scores(AHEAD)
    if att2:
        attention(1, side2)
    else:
        for step in sorted(side2):
            add(*side2[step])
    if att2:
        add(("values", 1, STEPS - 2))
        scores(2, late)
        add(("values", 1, STEPS - 1))
    if pro2:
        add(("qkv", 1, 0), ("qkv", 1, 1))
    if att2:
        add(("group_out", 1, GROUPS - 1))
        scores(2, late)
        add(("att_t", 1))
        scores(2, late)
        add(("project", 1), ("stats", 4))
        scores(2, late)
        add(("apply", 4))
        scores(2, late)
        add(("norm_t", 2), ("router",))
    if pro2:
        add(("head_rms", 0))
    scores(2, late)
    if att2:
        add(("route", 0), ("expert", 0), ("route", 1))
    scores(1, late)
    if att2:
        add(("expert", 1))
    if pro2:
        add(("head_rms", 1))
    scores(1, late)
    if att2:
        add(("expert", 2))
    if pro2:
        add(("head_rms", 2))
    scores(1, late)
    if att2:
        add(("expert", 3), ("expert", 4))
    scores(1, late)
    if pro2:
        add(("part1", 1))
    if att2:
        add(("expert", 5))
    scores(1, late)
    if pro2:
        add(("part2", 1))
    if att2:
        add(("expert", 6))
    if pro2:
        add(("q_rows", 1))
    scores(1, late)
    if att2:
        add(("expert", 7))
        scores(1, late)
        add(("down", 0))
        add(("down", 1))
        scores(1, late)
        add(("down", 2))
        add(("down", 3))
    scores(AHEAD, late)
    assert not tiles and not late
    return order


def first_tasks():
    return [("stats", 0), ("apply", 0), ("stats", 1), ("apply", 1), ("norm_t", 0), ("qkv", 0, 0), ("qkv", 0, 1),
            ("part1", 0), ("part2", 0), ("q_rows", 0), ("rows", 0, "k", 0), ("rows", 0, "q", 0), ("rows", 0, "k", 1),
            ("rows", 0, "q", 1)] + [("score", 0, n) for n in range(AHEAD)]


class Slot:

    def __init__(self, first, times, order, before):
        self.first, self.times, self.order = first, times, order
        self.base, self.per, self.index = dict(before), {}, {}
        for name, kinds in FILLS.items():
            fills = [(n, task) for n, task in enumerate(order) if task[0] in kinds]
            self.index[name] = {n: i for i, (n, _) in enumerate(fills)}
            self.per[name] = len(fills)
        assert times == 1 or all(self.per[n] % 2 == 0 for n in ("wide", "score"))

    def after(self):
        return {n: self.base[n] + self.times * self.per[n] for n in FILLS}


def slots():
    out, before = [], SETUP_FILLS
    for first, times, order in (
            (-1, 1, first_tasks()),
            (0, 1, tasks(True, False, True, True)),
            (1, SEQS - 2, tasks(True, True, True, True)),
            (SEQS - 1, 1, tasks(True, True, False, True)),
            (SEQS, 1, tasks(False, True, False, False))):
        out.append(Slot(first, times, order, before))
        before = out[-1].after()
    return out


SLOTS = slots()


class Now:

    def __init__(self, slot, j=None):
        self.slot, self.j, self.n = slot, j, 0

    def count(self, value, per):
        return value if self.j is None else self.j * per + value

    def fill(self, name, back=0):
        return self.slot.base[name] + self.slot.index[name][self.n - back], self.slot.per[name]

    def nth(self, name, task, plus=1):
        k = max(n for n in range(self.n + 1) if self.slot.order[n] == task)
        return self.count(self.slot.base[name] + self.slot.index[name][k] + plus, self.slot.per[name])

    def of_seq(self, ahead, per, c):
        return self.count((self.slot.first + ahead) * per + c, per)


def walk(engine, part):
    for slot in SLOTS:
        if slot.times == 1:
            now = Now(slot)
            for now.n, task in enumerate(slot.order):
                part(now, *task)
        else:
            with engine.Fori(0, slot.times) as j:
                now = Now(slot, j)
                for now.n, task in enumerate(slot.order):
                    part(now, *task)


PRE = {0: 1, 1: 0}
ATT = {0: 0, 1: -1}
STAT = (1, 1, 0, 0, -1)


def program(nc, t, out):
    with ExitStack() as ctx:
        def sb(name, shape, dt=F32):
            return ctx.enter_context(nc.sbuf_tensor(name, shape, dt))

        def psum(name, shape, dt=F32):
            return ctx.enter_context(nc.psum_tensor(name, shape, dt))

        def sem(name):
            return ctx.enter_context(nc.semaphore(name))

        room = sb("room", [P, 5 * 2 * TOKENS])
        stage = room[:, 0:NWT * P].rearrange("p (a n) -> p a n", n=P)
        wqkv_raw = room[:, NWT * P:NWT * P + 3 * D]
        spare = room[:, NWT * P + 3 * D:]
        mask_f = spare[:, 0:2 * P].rearrange("p (a n) -> p a n", a=2)
        gate_raw = spare[0:EXPERTS, 2 * P:3 * P]
        ones_row = spare[0:1, 3 * P:4 * P]
        row = spare[0:1, 4 * P:4 * P + D + 2 * HD]
        hid = {name: room[:, 2 * TOKENS * i:2 * TOKENS * (i + 1)].rearrange("p (a n) -> p a n", a=2)
               for i, name in enumerate(("h_e1", "h_l1", "h_l2", "h_e3", "h_e0"))}
        hid["h_l3"] = hid["h_l1"]
        h_e3d = sb("h_e3d", [P, TOKENS])
        wt = sb("wt", [P, NWT, P])
        wqkv1 = sb("wqkv1", [P, 3, D])
        wproj = sb("wproj", [P, D])
        gate_t = sb("gate_t", [P, EXPERTS])
        b_proj = sb("b_proj", [P, D])
        qk_w = sb("qk_w", [P, 2, HD])
        cols = sb("cols", [P, 4])
        id_f = sb("id_f", [P, P])
        id_b = sb("id_b", [P, P], BF16)
        mask_qk = sb("mask_qk", [P, P], BF16)
        mask_kq = sb("mask_kq", [P, P], BF16)
        before = sb("before", [P, EXPERTS, EXPERTS])
        behind = sb("behind", [P, EXPERTS, EXPERTS])
        eps = sb("eps", [P, 3, BLOCKS])
        credit = sb("credit", [P, 4])

        def token_tile(name):
            return sb(name, [P, BLOCKS, D])

        x, z, res1 = token_tile("x"), token_tile("z"), token_tile("res1")
        x1_new, y_new = token_tile("x1_new"), token_tile("y_new")
        x1, y = token_tile("x1"), token_tile("y")
        att = token_tile("att")
        att_t = sb("att_t", [P, TOKENS])
        n = [token_tile(f"n{i}") for i in range(2)] + [att]
        n_t = [sb(f"n_t{i}", [P, TOKENS]) for i in range(2)] + [att_t]
        bn = [sb(f"bn{i}", [P, BLOCKS, 6]) for i in range(5)]
        mv = [sb(f"mv{i}", [P, BLOCKS, 2]) for i in range(5)]
        ms = [sb(f"ms{i}", [P, BLOCKS]) for i in range(5)]
        ms2 = [sb(f"msq{i}", [P, BLOCKS]) for i in range(5)]
        rstd = [sb(f"rstd{i}", [P, BLOCKS]) for i in range(5)]
        qk = sb("qk", [P, 2, BLOCKS, D])
        rest = sb("rest", [P, 2, BLOCKS, D])
        hsum = sb("hsum", [P, 2 * BLOCKS * HEADS])
        hstep = sb("hstep", [P, 2 * BLOCKS * HEADS])
        hrstd = sb("hrstd", [P, 2 * BLOCKS * HEADS])
        part1 = sb("part1", [P, 2, BLOCKS, D], BF16)
        part2 = sb("part2", [P, 2, BLOCKS, D], BF16)
        q_tok = [sb(f"q_tok{i}", [P, BLOCKS, HEADS, ROWS], BF16) for i in range(2)]
        k_tok = sb("k_tok", [P, BLOCKS, HEADS, ROWS], BF16)
        k_t = [sb(f"k_t{i}", [P, PAIRS, TOKENS], BF16) for i in range(2)]
        q_t = [sb(f"q_t{i}", [P, 2, PAIRS, TOKENS], BF16) for i in range(2)]
        v_one = [sb(f"v_one{i}", [P, BLOCKS, HEADS, 32]) for i in range(2)]
        neg_max = sb("neg_max", [P, 2, BLOCKS, HEADS])
        probs = sb("probs", [P, RING, GROUP, TOKENS])
        o_t = sb("o_t", [P, TOKENS])
        rec = sb("rec", [P, BLOCKS, GROUP])
        lg = sb("lg", [P, BLOCKS, EXPERTS])
        lg_ok = sb("lg_ok", [P, BLOCKS, EXPERTS], U32)
        lgc = sb("lgc", [P, BLOCKS, EXPERTS])
        lmax = sb("lmax", [P, BLOCKS])
        lexp = sb("lexp", [P, BLOCKS, EXPERTS])
        prob = sb("prob", [P, BLOCKS, EXPERTS])
        ahead = sb("ahead", [P, BLOCKS, EXPERTS, EXPERTS])
        ahead2 = sb("ahead2", [P, BLOCKS, EXPERTS, EXPERTS])
        rank = sb("rank", [P, BLOCKS, EXPERTS])
        wts = sb("wts", [P, BLOCKS, EXPERTS])

        wide = [psum(f"wide{i}", [P, 2, 512]) for i in range(2)]
        score = [psum(f"score{i}", [P, 512]) for i in range(2)]
        pv = psum("pv", [P, 512])
        turn = psum("turn", [P, 512])
        turn_tok = turn[:, :].rearrange("p (t c) -> p t c", t=BLOCKS)

        w_loaded = sem("w_loaded")
        x_loaded = sem("x_loaded")
        out_stored = sem("out_stored")
        consts = sem("consts")
        w_ready = sem("w_ready")
        wide_full = sem("wide_full")
        wide_free = [sem(f"wide_free{i}") for i in range(2)]
        score_full = sem("score_full")
        score_free = sem("score_free")
        turn_full = sem("turn_full")
        turn_free = sem("turn_free")
        pv_done = sem("pv_done")
        ot_ready = sem("ot_ready")
        pool_step = sem("pool_step")
        stats_ready = [sem(f"stats_ready{i}") for i in range(5)]
        rstd_ready = [sem(f"rstd_ready{i}") for i in range(5)]
        n_ready = [sem(f"n_ready{i}") for i in range(3)]
        nt_ready = [sem(f"nt_ready{i}") for i in range(3)]
        z_ready = sem("z_ready")
        res1_ready = sem("res1_ready")
        y_ready = sem("y_ready")
        kept = sem("kept")
        u_ready = sem("u_ready")
        sum_ready = sem("sum_ready")
        qk_ready = [sem(f"qk_ready{i}") for i in range(2)]
        parts_ready = [sem(f"parts_ready{i}") for i in range(2)]
        q3_ready = [sem(f"q3_ready{i}") for i in range(2)]
        qtok_ready = [sem(f"qtok_ready{i}") for i in range(2)]
        ktok_ready = [sem(f"ktok_ready{i}") for i in range(2)]
        q_even = [sem(f"q_even{i}") for i in range(2)]
        max_ready = [sem(f"max_ready{i}") for i in range(2)]
        qmax_ready = [sem(f"qmax_ready{i}") for i in range(2)]
        att_t_ready = [sem(f"att_t_ready{i}") for i in range(2)]
        logits_ready = sem("logits_ready")
        lexp_ready = sem("lexp_ready")

        def wide_of(now, task=None):
            if task is None:
                first, per = now.fill("wide")
            else:
                k = max(i for i in range(now.n + 1) if now.slot.order[i] == task)
                first, per = now.slot.base["wide"] + now.slot.index["wide"][k], now.slot.per["wide"]
            return first % 2, now.count(first + 1, per), now.count(first // 2, per // 2), now.count(first // 2 + 1, per // 2)

        def score_of(now):
            first, per = now.fill("score")
            return first % 2, now.count(first + 1, per), now.count(first - 1, per)

        def turn_of(now):
            first, per = now.fill("turn")
            return now.count(first + 1, per), now.count(first, per)

        def step_of(now, layer, i):
            k = now.slot.order.index(("values", layer, i))
            return now.slot.base["pv"] + now.slot.index["pv"][k], now.slot.per["pv"]

        def flat(a):
            return a.rearrange("p a n -> p (a n)")

        W_LOADS = 26
        W_SETUP = SETUP_FILLS["wide"]
        block = ctx.enter_context(nc.Block())

        @block.sync
        def _(sp):
            def load(dst, src):
                sp.dma_start(dst, src).then_inc(w_loaded, 16)

            def store(s):
                slot = next(a for a in SLOTS if a.first <= s + 1 < a.first + a.times)
                last = slot.base["score"] + (s + 1 - slot.first) * slot.per["score"] + slot.index["score"][slot.order.index(("down", BLOCKS - 1))]
                sp.wait_ge(score_free, last + 1)
                sp.dma_start(dst[s], x1[:, :, :]).then_inc(out_stored, 16)

            load(wqkv_raw, t["L0_attn_w_qkv"])
            for i, name in enumerate(("ln_scale", "ln_bias")):
                load(cols[:, i:i + 1], t[f"L0_attn_{name}"].rearrange("(p a) -> p a", a=1))
            for i, name in enumerate(("n1_w", "n2_w")):
                load(cols[:, 2 + i:3 + i], t[f"L0_ffn_{name}"].rearrange("(p a) -> p a", a=1))
            load(row[:, 0:D], t["L0_attn_b_proj"].rearrange("(a n) -> a n", a=1))
            load(row[:, D:D + HD], t["L0_ffn_qn_w"].rearrange("(a n) -> a n", a=1))
            load(row[:, D + HD:], t["L0_ffn_kn_w"].rearrange("(a n) -> a n", a=1))
            load(wproj[:, :], t["L0_attn_w_proj"])
            load(gate_raw[:, :], t["L0_ffn_gate_w"])
            for i, name in enumerate(("wq", "wk", "wv", "wo")):
                load(stage[:, i, :], t[f"L0_ffn_{name}"])
            load(stage[:, E3_DOWN, :], t["L0_ffn_e3_down"])
            for at, name in ((E0_UP, "e0_up"), (E1_W1, "e1_w1"), (E1_W2, "e1_w2"), (E2_L1, "e2_l1"), (E3_UP, "e3_up")):
                sp.dma_start(stage[:, at:at + 2, :], t[f"L0_ffn_{name}"].rearrange("(a p) c -> p a c", p=P)).then_inc(w_loaded, 16)
            for at, name in ((E2_L2, "e2_l2"), (E2_L3, "e2_l3")):
                sp.dma_start(stage[:, at:at + 4, :].rearrange("p (a k) c -> p a (k c)", a=2),
                             t[f"L0_ffn_{name}"].rearrange("(a p) n -> p a n", p=P)).then_inc(w_loaded, 16)
            for at, name in ((E0_DN, "e0_down"), (E1_DN, "e1_down"), (E2_DN, "e2_l4"), (E3_DN, "e3_out")):
                load(stage[:, at:at + 2, :].rearrange("p k c -> p (k c)"), t[f"L0_ffn_{name}"])
            src = t["L0_attn_z"].rearrange("b (t p) d -> b p t d", p=P)
            dst = out.rearrange("b (t p) d -> b p t d", p=P)
            sp.dma_start(x[:, :, :], src[0]).then_inc(x_loaded, 16)
            for s in range(SEQS):
                if s + 1 < SEQS:
                    sp.wait_ge(res1_ready, s + 1)
                    sp.dma_start(x[:, :, :], src[s + 1]).then_inc(x_loaded, 16)
                if s > 0:
                    store(s - 1)
            store(SEQS - 1)
            sp.wait_ge(out_stored, 16 * (SEQS + 1))
        @block.gpsimd
        def _(pool):
            steps = [0]

            def link(ins):
                steps[0] += 1
                ins.then_inc(pool_step, 1)
                pool.wait_ge(pool_step, steps[0])

            nc.gpsimd.memset(id_f[:, :], 0.0)
            nc.gpsimd.memset(mask_f[:, :, :], 0.0)
            nc.gpsimd.memset(before[:, :, :], 1.0)
            for i, value in enumerate((LN_EPS, RMS_EPS, -0.5)):
                nc.gpsimd.memset(eps[:, i, :], value)
            nc.gpsimd.memset(behind[:, :, :], 1.0)
            link(nc.gpsimd.memset(ones_row[:, :], 1.0))
            nc.gpsimd.affine_select(out=id_f[:, :], in_=id_f[:, :], compare_op=ALU.not_equal, fill=1.0,
                                    base=0, pattern=[[-1, P]], channel_multiplier=1)
            nc.gpsimd.affine_select(out=mask_f[:, 0, :], in_=mask_f[:, 0, :], compare_op=ALU.is_ge, fill=MASKED,
                                    base=0, pattern=[[-1, P]], channel_multiplier=1)
            nc.gpsimd.affine_select(out=mask_f[:, 1, :], in_=mask_f[:, 1, :], compare_op=ALU.is_ge, fill=MASKED,
                                    base=0, pattern=[[1, P]], channel_multiplier=-1)
            nc.gpsimd.affine_select(out=before[:, :, :], in_=before[:, :, :], compare_op=ALU.is_gt, fill=0.0,
                                    base=0, pattern=[[1, EXPERTS], [-1, EXPERTS]], channel_multiplier=0)
            link(nc.gpsimd.affine_select(out=behind[:, :, :], in_=behind[:, :, :], compare_op=ALU.is_gt, fill=0.0,
                                         base=0, pattern=[[-1, EXPERTS], [1, EXPERTS]], channel_multiplier=0))
            nc.gpsimd.tensor_copy(id_b[:, :], id_f[:, :])
            nc.gpsimd.tensor_copy(mask_qk[:, :], mask_f[:, 0, :])
            nc.gpsimd.tensor_copy(mask_kq[:, :], mask_f[:, 1, :]).then_inc(consts, 1)
            for i in range(2):
                nc.gpsimd.memset(q_tok[i][:, :, :, :], 0.0)
                nc.gpsimd.memset(q_t[i][:, :, :, :], 0.0)
                nc.gpsimd.memset(v_one[i][:, :, :, :], 0.0)
            link(nc.gpsimd.memset(k_tok[:, :, :, :], 0.0))
            for i in range(2):
                nc.gpsimd.memset(v_one[i][:, :, :, HD:HD + 1], 1.0)
            nc.gpsimd.memset(k_tok[:, :, :, MAX_ROW:MAX_ROW + 2], 1.0).then_inc(consts, 1)
            nc.gpsimd.memset(credit[:, 1:2], 0.0).then_inc(out_stored, 16)
            pool.wait_ge(w_ready, 3)

            def add(out, a, b):
                return nc.gpsimd.tensor_tensor(out, a, b, ALU.add)

            def part(now, name, *args):
                if name == "stats":
                    w = args[0]
                    pool.wait_ge(stats_ready[w], now.of_seq(STAT[w], 1, 1))
                    if w >= 3:
                        nc.gpsimd.tensor_tensor(ms2[w][:, :], mv[w][:, :, 0], mv[w][:, :, 0], ALU.mult)
                        pool.drain()
                        add(ms2[w][:, :], ms2[w][:, :], mv[w][:, :, 1])
                        pool.drain()
                        add(ms[w][:, :], ms2[w][:, :], eps[:, 1, :])
                    else:
                        add(ms[w][:, :], mv[w][:, :, 1], eps[:, 0, :])
                    pool.drain()
                    nc.gpsimd.tensor_tensor(rstd[w][:, :], ms[w][:, :], eps[:, 2, :], ALU.pow).then_inc(rstd_ready[w], 1)
                elif name == "norm_t" and args[0] == 0:
                    pool.wait_ge(n_ready[0], now.of_seq(1, 1, 1))
                    add(res1[:, :, :], x[:, :, :], z[:, :, :])
                    pool.drain()
                    add(res1[:, :, :], res1[:, :, :], b_proj[:, :].unsqueeze(1).broadcast_to([P, BLOCKS, D])).then_inc(res1_ready, 1)
                elif name == "keep_y":
                    pool.wait_ge(out_stored, now.of_seq(-1, 16, 16))
                    pool.wait_ge(y_ready, now.of_seq(-1, 1, 1))
                    add(credit[:, 3:4], eps[:, 0, 0:1], eps[:, 0, 0:1])
                    nc.gpsimd.tensor_copy(x1[:, :, :], x1_new[:, :, :])
                    nc.gpsimd.tensor_copy(y[:, :, :], y_new[:, :, :]).then_inc(kept, 1)
                elif name == "q_rows":
                    layer = args[0]
                    k_rows = k_tok[:, :, :, :].rearrange("p t h r -> p (t h) r")[:, :, 0:MAX_ROW].rearrange(
                        "p g (s d) -> p g s d", d=HD)
                    p1, p2, r = (a[:, 1, :, :].rearrange("p t (h d) -> p (t h) d", d=HD) for a in (part1, part2, rest))
                    G = BLOCKS * HEADS
                    pool.wait_ge(parts_ready[layer], now.of_seq(PRE[layer], 2, 2))
                    nc.gpsimd.tensor_tensor(k_rows[:, :, 5, :], r, p2, ALU.subtract)
                    nc.gpsimd.tensor_copy(k_rows[:, :, 0:5:2, :], p1.unsqueeze(2).broadcast_to([P, G, 3, HD]))
                    nc.gpsimd.tensor_copy(k_rows[:, :, 1:4:2, :], p2.unsqueeze(2).broadcast_to([P, G, 2, HD])).then_inc(ktok_ready[layer], 1)
                elif name == "project" and args[0] == 1:
                    pool.wait_ge(u_ready, now.of_seq(-1, 1, 1))
                    add(x1[:, :, :], x1[:, :, :], y[:, :, :]).then_inc(sum_ready, 1)

            walk(pool, part)

        @block.scalar
        def _(act):
            act.wait_ge(w_loaded, 16 * W_LOADS)
            raw = wqkv_raw.rearrange("p (n j) -> p j n", j=3)
            nc.scalar.activation(wqkv1[:, 0, :], raw[:, 0, :], ACT.Copy, scale=SCALE)
            nc.scalar.activation(wqkv1[:, 1:3, :], raw[:, 1:3, :], ACT.Copy).then_inc(w_ready, 1)
            for u in range(0, W_SETUP, 2):
                act.wait_ge(wide_full, u + 1)
                nc.scalar.activation(wt[:, 8 * u:8 * u + 8, :].rearrange("p (a c) n -> p a (c n)", a=2),
                                     wide[0][:, :, :], ACT.Copy).then_inc(wide_free[0], 1)

            HIDDEN = (("h_e1", ACT.Silu), None, ("h_l1", ACT.Gelu), ("h_e3d", ACT.Gelu), ("h_l2", ACT.Gelu),
                      ("h_e3", ACT.Gelu), ("h_l3", ACT.Gelu), ("h_e0", ACT.Gelu))

            def part(now, name, *args):
                if name == "norm_t":
                    w = args[0]
                    act.wait_ge(turn_full, turn_of(now)[0])
                    if w == 0:
                        ins = nc.scalar.activation(n_t[0][:, :], turn[:, :], ACT.Identity, scale=cols[:, 0:1], bias=cols[:, 1:2])
                    else:
                        ins = nc.scalar.activation(n_t[w][:, :], turn[:, :], ACT.Copy, scale=cols[:, w + 1:w + 2])
                    ins.then_inc(turn_free, 1)
                elif name == "qkv":
                    layer, u = args
                    buf, full, _, _ = wide_of(now)
                    act.wait_ge(wide_full, full)
                    nc.scalar.activation(qk[:, :, 2 * u:2 * u + 2, :],
                                         wide[buf][:, :, 0:2 * D].rearrange("p t (a n) -> p a t n", a=2), ACT.Copy).then_inc(qk_ready[layer], 1)
                    for k in range(2):
                        ins = nc.scalar.activation(v_one[layer][:, 2 * u + k, :, 0:HD],
                                                   wide[buf][:, k, 2 * D:3 * D].rearrange("p (h d) -> p h d", d=HD), ACT.Copy)
                    ins.then_inc(wide_free[buf], 1)
                elif name == "q_rows":
                    layer = args[0]
                    q_rows = q_tok[layer][:, :, :, :].rearrange("p t h r -> p (t h) r")[:, :, 0:MAX_ROW].rearrange(
                        "p g (s d) -> p g s d", d=HD)
                    p1, p2 = (a[:, 0, :, :].rearrange("p t (h d) -> p (t h) d", d=HD) for a in (part1, part2))
                    G = BLOCKS * HEADS
                    act.wait_ge(parts_ready[layer], now.of_seq(PRE[layer], 2, 2))
                    nc.scalar.activation(q_rows[:, :, 0:2, :], p1.unsqueeze(2).broadcast_to([P, G, 2, HD]), ACT.Copy)
                    nc.scalar.activation(q_rows[:, :, 5, :], p1, ACT.Copy)
                    nc.scalar.activation(q_rows[:, :, 2:4, :], p2.unsqueeze(2).broadcast_to([P, G, 2, HD]), ACT.Copy).then_inc(qtok_ready[layer], 1)
                elif name == "rows":
                    layer, what, half = args
                    buf, full, _, _ = wide_of(now)
                    act.wait_ge(wide_full, full)
                    src = flat(wide[buf][:, :, :]).bitcast(BF16)
                    if what == "k":
                        nc.scalar.activation(flat(k_t[layer][:, 4 * half:4 * half + 4, :]), src, ACT.Copy).then_inc(wide_free[buf], 1)
                    else:
                        nc.scalar.activation(flat(q_t[layer][0:ROWS, 0, 4 * half:4 * half + 4, :]), src[0:ROWS], ACT.Copy)\
                            .then_inc(q_even[layer], 1)
                elif name == "max_rows":
                    layer, g = args
                    act.wait_ge(turn_full, turn_of(now)[0])
                    for k in range(2):
                        ins = nc.scalar.activation(flat(q_t[layer][ROWS * k:ROWS * (k + 1), k, 2 * g:2 * g + 2, :]),
                                                   turn[ROWS * k:ROWS * (k + 1), :].bitcast(BF16), ACT.Copy)
                    ins.then_inc(turn_free, 1)
                elif name == "shifted":
                    layer, i, half = args
                    buf, full, _, _ = wide_of(now)
                    first, per = step_of(now, layer, i)
                    if half == 0 and first >= RING:
                        act.wait_ge(pv_done, now.count(first - RING + 1, per))
                    act.wait_ge(wide_full, full)
                    c0 = P * (i % BLOCKS) if layer else 0
                    nc.scalar.activation(probs[:, i % RING, 2 * half:2 * half + 2, c0:], wide[buf][:, :, c0:],
                                         ACT.Exp).then_inc(wide_free[buf], 1)
                elif name == "values" and args[1] % BLOCKS == BLOCKS - 1:
                    first, per = step_of(now, *args)
                    act.wait_ge(pv_done, now.count(first + 1, per))
                    nc.scalar.activation(o_t[:, :], pv[:, :], ACT.Copy).then_inc(ot_ready, 1)
                elif name == "att_t":
                    act.wait_ge(turn_full, turn_of(now)[0])
                    nc.scalar.activation(att_t[:, :], turn[:, :], ACT.Copy).then_inc(turn_free, 1)
                elif name == "route" and args[0] == 0:
                    act.wait_ge(logits_ready, now.of_seq(-1, 1, 1))
                    nc.scalar.activation(lexp[:, :, :], lgc[:, :, :], ACT.Exp).then_inc(lexp_ready, 1)
                elif name == "expert" and HIDDEN[args[0]]:
                    target, fn = HIDDEN[args[0]]
                    buf, full, _, _ = wide_of(now)
                    act.wait_ge(wide_full, full)
                    if target == "h_e3d":
                        ins = nc.scalar.activation(h_e3d[:, :], wide[buf][:, 0, :], fn)
                    else:
                        ins = nc.scalar.activation(hid[target], wide[buf][:, :, :], fn)
                    ins.then_inc(wide_free[buf], 1)

            walk(act, part)

        @block.vector
        def _(dve):
            nc.vector.memset(credit[:, 0:1], 0.0).then_inc(score_free, 2)
            nc.vector.memset(credit[:, 2:3], 0.0).then_inc(score_full, 2)
            for u in range(1, W_SETUP, 2):
                dve.wait_ge(wide_full, u + 1)
                m = min(8, NWT - 8 * u)
                nc.vector.tensor_copy(wt[:, 8 * u:8 * u + m, :].rearrange("p a n -> p (a n)"),
                                      wide[1][:, :, :].rearrange("p a n -> p (a n)")[:, 0:m * P]).then_inc(wide_free[1], 1)
            dve.wait_ge(turn_full, 1)
            nc.vector.tensor_copy(gate_t[:, :], turn[:, 0:EXPERTS])
            nc.vector.tensor_copy(b_proj[:, :], turn[:, 128:256]).then_inc(w_ready, 1)
            rows = turn[:, 256:256 + 2 * HD].rearrange("p (a d) -> p a d", a=2)
            nc.vector.tensor_copy(qk_w[:, 1, :], rows[:, 1, :])
            nc.vector.tensor_scalar(qk_w[:, 0, :], rows[:, 0, :], SCALE, None, ALU.mult).then_inc(turn_free, 1)
            nc.vector.memset(lgc[:, :, :], 0.0).then_inc(w_ready, 1)

            def settle():
                dve.drain()

            def part(now, name, *args):
                if name == "stats":
                    w = args[0]
                    settle()
                    if w == 0:
                        dve.wait_ge(x_loaded, now.of_seq(1, 16, 16))
                    for k in range(BLOCKS):
                        nc.vector.bn_stats(bn[w][:, k, :], NORM[w][0][:, k, :])
                    settle()
                    for k in range(BLOCKS):
                        ins = nc.vector.bn_aggr(mv[w][:, k, :], bn[w][:, k, :])
                    ins.then_inc(stats_ready[w], 1)
                elif name == "apply":
                    w = args[0]
                    src, dst = NORM[w]
                    dve.wait_ge(rstd_ready[w], now.of_seq(STAT[w], 1, 1))
                    for k in range(BLOCKS):
                        if w < 3:
                            ins = nc.vector.tensor_scalar(dst[:, k, :], src[:, k, :], mv[w][:, k, 0:1], rstd[w][:, k:k + 1],
                                                          ALU.subtract, ALU.mult)
                        else:
                            ins = nc.vector.tensor_scalar(dst[:, k, :], src[:, k, :], rstd[w][:, k:k + 1], None, ALU.mult)
                    ins.then_inc({0: z_ready, 1: n_ready[0], 2: y_ready, 3: n_ready[1], 4: n_ready[2]}[w], 1)
                elif name == "head_rms":
                    qk_all = qk[:, :, :, :].rearrange("p a t n -> p (a t n)")
                    heads = qk_all.rearrange("p (g d) -> p g d", d=HD)
                    if args[0] == 0:
                        dve.wait_ge(qk_ready[1], now.of_seq(0, 2, 2))
                        sq = rest[:, :, :, :].rearrange("p a t n -> p (a t n)")
                        nc.vector.tensor_tensor(sq, qk_all, qk_all, ALU.mult)
                        settle()
                        nc.vector.tensor_reduce(hsum[:, :], sq.rearrange("p (g d) -> p g d", d=HD), AX.X, ALU.add)
                        settle()
                        nc.vector.tensor_scalar(hsum[:, :], hsum[:, :], 1.0 / HD, RMS_EPS, ALU.mult, ALU.add)
                    elif args[0] == 1:
                        nc.vector.tensor_scalar(hrstd[:, :].bitcast(U32), hsum[:, :].bitcast(U32), -0.5, 1597463007.0, ALU.mult, ALU.add)
                        settle()
                        for _ in range(3):
                            nc.vector.scalar_tensor_tensor(out=hstep[:, :], in0=hsum[:, :], scalar=-0.5, in1=hrstd[:, :],
                                                           op0=ALU.mult, op1=ALU.mult)
                            settle()
                            nc.vector.tensor_tensor(hstep[:, :], hstep[:, :], hrstd[:, :], ALU.mult)
                            settle()
                            nc.vector.scalar_tensor_tensor(out=hrstd[:, :], in0=hstep[:, :], scalar=1.5, in1=hrstd[:, :],
                                                           op0=ALU.add, op1=ALU.mult)
                            settle()
                    else:
                        nc.vector.tensor_tensor(heads, heads, hrstd[:, :].unsqueeze(2).broadcast_to([P, 2 * BLOCKS * HEADS, HD]), ALU.mult)
                        settle()
                        both = qk_all.rearrange("p (a g d) -> p a g d", a=2, d=HD)
                        nc.vector.tensor_tensor(both, both, qk_w[:, :, :].unsqueeze(2).broadcast_to([P, 2, BLOCKS * HEADS, HD]), ALU.mult)
                    settle()
                elif name == "part1":
                    layer = args[0]
                    dve.wait_ge(qk_ready[layer], now.of_seq(PRE[layer], 2, 2))
                    f1, qk_all, r = (a[:, :, :, :].rearrange("p a t n -> p (a t n)") for a in (part1, qk, rest))
                    nc.vector.tensor_copy(f1, qk_all)
                    settle()
                    nc.vector.tensor_tensor(r, qk_all, f1, ALU.subtract).then_inc(parts_ready[layer], 1)
                elif name == "part2":
                    layer = args[0]
                    f2, r = (a[:, :, :, :].rearrange("p a t n -> p (a t n)") for a in (part2, rest))
                    settle()
                    nc.vector.tensor_copy(f2, r).then_inc(parts_ready[layer], 1)
                    settle()
                    nc.vector.memset(q_tok[layer][:, :, :, MAX_ROW:MAX_ROW + 2], 0.0)
                    nc.vector.tensor_tensor(q_tok[layer][:, :, :, 4 * HD:5 * HD],
                                            rest[:, 0, :, :].rearrange("p t (h d) -> p t h d", d=HD),
                                            part2[:, 0, :, :].rearrange("p t (h d) -> p t h d", d=HD), ALU.subtract).then_inc(q3_ready[layer], 1)
                elif name == "rows" and args[1] == "q":
                    layer, _, half = args
                    buf, full, _, _ = wide_of(now)
                    dve.wait_ge(wide_full, full)
                    nc.vector.tensor_copy(flat(q_t[layer][ROWS:, 1, 4 * half:4 * half + 4, :]),
                                          flat(wide[buf][ROWS:, :, :]).bitcast(BF16)).then_inc(wide_free[buf], 1)
                elif name == "score":
                    layer, tile = args
                    h, qb = divmod(tile, BLOCKS)
                    width = P * (qb + 1) if layer else TOKENS
                    buf, full, free = score_of(now)
                    dve.wait_ge(score_full, full)
                    nc.vector.tensor_reduce(neg_max[:, layer, qb, h:h + 1], score[buf][:, 0:width], AX.X, ALU.max,
                                            negate=True).then_inc(score_free, 1)
                    if tile % GTILES == GTILES - 1:
                        g = h // GROUP
                        hs = slice(GROUP * g, GROUP * (g + 1))
                        settle()
                        nc.vector.tensor_copy(q_tok[layer][:, :, hs, MAX_ROW], neg_max[:, layer, :, hs])
                        settle()
                        nc.vector.tensor_tensor(q_tok[layer][:, :, hs, MAX_ROW + 1], neg_max[:, layer, :, hs],
                                                q_tok[layer][:, :, hs, MAX_ROW], ALU.subtract).then_inc(max_ready[layer], 1)
                elif name == "group_out":
                    layer, g = args
                    dve.wait_ge(turn_full, turn_of(now)[0])
                    o = turn[:, :].rearrange("p (t j r) -> p t j r", t=BLOCKS, j=GROUP)
                    nc.vector.reciprocal(rec[:, :, :], o[:, :, :, HD])
                    settle()
                    nc.vector.tensor_tensor(att[:, :, GROUP * HD * g:GROUP * HD * (g + 1)].rearrange("p t (j d) -> p t j d", d=HD),
                                            o[:, :, :, 0:HD], rec[:, :, :].unsqueeze(3).broadcast_to([P, BLOCKS, GROUP, HD]),
                                            ALU.mult).then_inc(turn_free, 1)
                elif name == "project":
                    buf, full, free = score_of(now)
                    if args[0] == 0:
                        dve.wait_ge(res1_ready, now.of_seq(0, 1, 1))
                        if now.slot.first > 0:
                            dve.wait_ge(kept, now.of_seq(-1, 1, 1))
                        dve.wait_ge(score_full, full)
                        nc.vector.tensor_tensor(x1_new[:, :, :], score[buf][:, :].rearrange("p (t n) -> p t n", t=BLOCKS),
                                                res1[:, :, :], ALU.add).then_inc(score_free, 1)
                    else:
                        dve.wait_ge(kept, now.of_seq(-1, 1, 1))
                        dve.wait_ge(score_full, full)
                        nc.vector.tensor_tensor(y[:, :, KEPT:], score[buf][:, 0:BLOCKS * OUTC].rearrange("p (t n) -> p t n", t=BLOCKS),
                                                y[:, :, KEPT:], ALU.add).then_inc(score_free, 1)
                        settle()
                        nc.vector.memset(credit[:, 0:1], 0.0).then_inc(u_ready, 1)
                elif name == "route" and args[0] == 0:
                    dve.wait_ge(turn_full, router_full(now))
                    nc.vector.tensor_copy(lg[:, :, :], turn[:, 0:BLOCKS * EXPERTS].rearrange("p (t e) -> p t e", e=EXPERTS)).then_inc(turn_free, 1)
                    settle()
                    nc.vector.memset(lgc[:, :, :], 0.0)
                    nc.vector.tensor_tensor(lg_ok[:, :, :], lg[:, :, :], lg[:, :, :], ALU.is_equal)
                    settle()
                    nc.vector.copy_predicated(lgc[:, :, :], lg_ok[:, :, :], lg[:, :, :])
                    settle()
                    nc.vector.tensor_scalar(lg[:, :, :], lgc[:, :, :], -F32_MAX, F32_MAX, ALU.max, ALU.min)
                    settle()
                    nc.vector.tensor_reduce(lmax[:, :], lg[:, :, :], AX.X, ALU.max)
                    settle()
                    nc.vector.tensor_tensor(lgc[:, :, :], lg[:, :, :], lmax[:, :].unsqueeze(2).broadcast_to([P, BLOCKS, EXPERTS]),
                                            ALU.subtract).then_inc(logits_ready, 1)
                elif name == "route":
                    dve.wait_ge(lexp_ready, now.of_seq(-1, 1, 1))
                    four = [P, BLOCKS, EXPERTS, EXPERTS]
                    nc.vector.tensor_reduce(lmax[:, :], lexp[:, :, :], AX.X, ALU.add)
                    settle()
                    nc.vector.reciprocal(lmax[:, :], lmax[:, :])
                    settle()
                    nc.vector.tensor_tensor(prob[:, :, :], lexp[:, :, :], lmax[:, :].unsqueeze(2).broadcast_to([P, BLOCKS, EXPERTS]), ALU.mult)
                    settle()
                    p_i = prob[:, :, :].unsqueeze(2).broadcast_to(four)
                    p_j = prob[:, :, :].unsqueeze(3).broadcast_to(four)
                    nc.vector.tensor_tensor(ahead[:, :, :, :], p_i, p_j, ALU.is_ge)
                    nc.vector.tensor_tensor(ahead2[:, :, :, :], p_i, p_j, ALU.is_gt)
                    settle()
                    nc.vector.tensor_tensor(ahead[:, :, :, :], ahead[:, :, :, :], before[:, :, :].unsqueeze(1).broadcast_to(four), ALU.mult)
                    nc.vector.tensor_tensor(ahead2[:, :, :, :], ahead2[:, :, :, :], behind[:, :, :].unsqueeze(1).broadcast_to(four), ALU.mult)
                    settle()
                    nc.vector.tensor_tensor(ahead[:, :, :, :], ahead[:, :, :, :], ahead2[:, :, :, :], ALU.add)
                    settle()
                    nc.vector.tensor_reduce(rank[:, :, :], ahead[:, :, :, :], AX.X, ALU.add)
                    settle()
                    nc.vector.scalar_tensor_tensor(out=wts[:, :, :], in0=rank[:, :, :], scalar=1.5, in1=prob[:, :, :],
                                                        op0=ALU.is_lt, op1=ALU.mult)
                    settle()
                    nc.vector.tensor_reduce(lmax[:, :], wts[:, :, :], AX.X, ALU.add)
                    settle()
                    nc.vector.tensor_scalar(lmax[:, :], lmax[:, :], 1e-8, None, ALU.add)
                    settle()
                    nc.vector.reciprocal(lmax[:, :], lmax[:, :])
                    settle()
                    nc.vector.tensor_tensor(wts[:, :, :], wts[:, :, :], lmax[:, :].unsqueeze(2).broadcast_to([P, BLOCKS, EXPERTS]), ALU.mult)
                    settle()
                elif name == "expert" and args[0] == 1:
                    buf, full, _, _ = wide_of(now)
                    other, _, _, used = wide_of(now, ("expert", 0))
                    dve.wait_ge(wide_full, full)
                    dve.wait_ge(wide_free[other], used)
                    nc.vector.tensor_tensor(hid["h_e1"], hid["h_e1"], wide[buf][:, :, :], ALU.mult).then_inc(wide_free[buf], 1)
                elif name == "down":
                    k = args[0]
                    buf, full, free = score_of(now)
                    if k == 0:
                        dve.wait_ge(sum_ready, now.of_seq(-1, 1, 1))
                    dve.wait_ge(score_full, full)
                    for e in range(EXPERTS):
                        ins = nc.vector.scalar_tensor_tensor(
                            out=x1[:, k, KEPT:], in0=score[buf][:, OUTC * e:OUTC * (e + 1)], scalar=wts[:, k, e:e + 1],
                            in1=x1[:, k, KEPT:], op0=ALU.mult, op1=ALU.add)
                        if e < EXPERTS - 1:
                            settle()
                    ins.then_inc(score_free, 1)

            NORM = ((x, z), (z, n[0]), (x1_new, y_new), (y_new, n[1]), (y, n[2]))

            def router_full(now):
                k = max(i for i in range(now.n) if now.slot.order[i] == ("router",))
                return now.count(now.slot.base["turn"] + now.slot.index["turn"][k] + 1, now.slot.per["turn"])

            walk(dve, part)

        @block.tensor
        def _(pe):
            pe.wait_ge(w_loaded, 16 * W_LOADS)
            pe.wait_ge(consts, 1)
            for u in range(W_SETUP):
                if u >= 2:
                    pe.wait_ge(wide_free[u % 2], u // 2)
                for k in range(8 * u, min(8 * u + 8, NWT)):
                    ins = nc.tensor.transpose(wide[u % 2][:, k % 8 // 4, k % 4 * P:k % 4 * P + P], stage[:, k, :], id_f[:, :])
                ins.then_inc(wide_full, 1)
            nc.tensor.transpose(turn[:, 0:EXPERTS], gate_raw[:, :], id_f[0:EXPERTS, 0:EXPERTS])
            nc.tensor.matmul(turn[:, 128:128 + D + 2 * HD], ones_row[:, :], row[:, :], start=True, stop=True).then_inc(turn_full, 1)
            pe.wait_ge(w_ready, 3)
            pe.wait_ge(consts, 2)

            def by_token(src, now):
                full, free = turn_of(now)
                pe.wait_ge(turn_free, free)
                for k in range(BLOCKS):
                    ins = nc.tensor.transpose(turn[:, P * k:P * (k + 1)], src(k), id_f[:, :])
                ins.then_inc(turn_full, 1)

            def turn_read(now, task):
                k = max(i for i in range(now.n) if now.slot.order[i] == task)
                pe.wait_ge(turn_free, now.count(now.slot.base["turn"] + now.slot.index["turn"][k] + 1, now.slot.per["turn"]))

            shared = {}

            def wide_wait(now):
                buf, _, free, _ = wide_of(now)
                pe.wait_ge(wide_free[buf], free)
                if buf in shared:
                    pe.wait_ge(*shared.pop(buf))
                return buf

            def written(now, task):
                buf, _, _, used = wide_of(now, task)
                pe.wait_ge(wide_free[buf], used)

            EXPERT_IN = ((E1_W1, 2, None), (E1_W2, 2, None), (E2_L1, 2, None), (E3_DOWN, 1, None), (E2_L2, 2, "h_l1"),
                         (E3_UP, 2, "h_e3d"), (E2_L3, 2, "h_l2"), (E0_UP, 2, None))
            EXPERT_NEEDS = {4: 2, 5: 3, 6: 4}

            def part(now, name, *args):
                if name == "norm_t":
                    w = args[0]
                    pe.wait_ge(n_ready[w], now.of_seq((1, 0, -1)[w], 1, 1))
                    by_token(lambda k: n[w][:, k, :], now)
                elif name == "qkv":
                    layer, u = args
                    if u == 0:
                        turn_read(now, ("norm_t", layer))
                    buf = wide_wait(now)
                    w_in = wqkv1[:, :, :] if layer == 0 else wt[:, WQKV2:WQKV2 + 3, :]
                    for k in range(2):
                        kb = 2 * u + k
                        ins = nc.tensor.matmul(wide[buf][:, k, 0:3 * D], n_t[layer][:, P * kb:P * (kb + 1)], flat(w_in),
                                               start=True, stop=True)
                    ins.then_inc(wide_full, 1)
                elif name == "rows":
                    layer, what, half = args
                    seq = 1 if layer == 0 else -1
                    src = k_tok if what == "k" else q_tok[layer]
                    if what == "k":
                        pe.wait_ge(ktok_ready[layer], now.of_seq(seq, 1, 1))
                    else:
                        pe.wait_ge(qtok_ready[layer], now.of_seq(seq, 1, 1))
                        pe.wait_ge(q3_ready[layer], now.of_seq(seq, 1, 1))
                    buf = wide_wait(now)
                    dst = flat(wide[buf][:, :, :]).bitcast(BF16)
                    for a in range(4):
                        pair = 4 * half + a
                        for k in range(BLOCKS):
                            ins = nc.tensor.transpose(dst[:, TOKENS * a + P * k:TOKENS * a + P * (k + 1)],
                                                      src[:, k, 2 * pair:2 * pair + 2, :].rearrange("p h r -> p (h r)"), id_b[:, :])
                    ins.then_inc(wide_full, 1)
                    if what == "q":
                        shared[buf] = (q_even[layer], now.of_seq(seq, 2, half + 1))
                elif name == "score":
                    layer, tile = args
                    h, qb = divmod(tile, BLOCKS)
                    width = P * (qb + 1) if layer else TOKENS
                    if tile == 0:
                        written(now, ("rows", layer, "k", 1))
                        written(now, ("rows", layer, "q", 1))
                        pe.wait_ge(q_even[layer], now.of_seq(1 if layer == 0 else -1, 2, 2))
                    buf, _, free = score_of(now)
                    pe.wait_ge(score_free, free)
                    ins = nc.tensor.matmul(score[buf][:, 0:width], q_t[layer][:, h % 2, h // 2, P * qb:P * (qb + 1)],
                                           k_t[layer][:, h // 2, 0:width], start=True, stop=not layer)
                    if layer:
                        ins = nc.tensor.matmul(score[buf][:, P * qb:width], id_b[:, :], mask_qk[:, :], start=False, stop=True)
                    ins.then_inc(score_full, 1)
                elif name == "max_rows":
                    layer, g = args
                    pe.wait_ge(max_ready[layer], now.of_seq(ATT[layer], GROUPS, g + 1))
                    pe.wait_ge(turn_free, turn_of(now)[1])
                    dst = turn[:, :].bitcast(BF16)
                    for a in range(2):
                        for k in range(BLOCKS):
                            h = GROUP * g + 2 * a
                            ins = nc.tensor.transpose(dst[:, TOKENS * a + P * k:TOKENS * a + P * (k + 1)],
                                                      q_tok[layer][:, k, h:h + 2, :].rearrange("p h r -> p (h r)"), id_b[:, :])
                    ins.then_inc(turn_full, 1)
                elif name == "shifted":
                    layer, i, half = args
                    g, kb = divmod(i, BLOCKS)
                    if kb == 0 and half == 0:
                        turn_read(now, ("max_rows", layer, g))
                    buf = wide_wait(now)
                    pair = 2 * g + half
                    c0 = P * kb if layer else 0
                    for k in range(2):
                        ins = nc.tensor.matmul(wide[buf][:, k, c0:], k_t[layer][:, pair, P * kb:P * (kb + 1)],
                                               q_t[layer][:, k, pair, c0:], start=True, stop=not layer)
                        if layer:
                            ins = nc.tensor.matmul(wide[buf][:, k, c0:c0 + P], id_b[:, :], mask_kq[:, :], start=False, stop=True)
                    ins.then_inc(wide_full, 1)
                elif name == "values":
                    layer, i = args
                    g, kb = divmod(i, BLOCKS)
                    c0 = P * kb if layer else 0
                    written(now, ("shifted", layer, i, 0))
                    written(now, ("shifted", layer, i, 1))
                    first, per = step_of(now, layer, i)
                    if kb == 0 and first > 0:
                        pe.wait_ge(ot_ready, now.count(first // BLOCKS, per // BLOCKS))
                    for j in range(GROUP):
                        ins = nc.tensor.matmul(pv[32 * j:32 * j + 32, c0:], v_one[layer][:, kb, GROUP * g + j, :],
                                               probs[:, i % RING, j, c0:], start=(kb == 0), stop=(kb == BLOCKS - 1),
                                               tile_position=(0, 32 * j))
                    ins.then_inc(pv_done, 1)
                elif name == "group_out":
                    layer, g = args
                    first, per = step_of(now, layer, BLOCKS * g + BLOCKS - 1)
                    pe.wait_ge(ot_ready, now.count(first // BLOCKS + 1, per // BLOCKS))
                    by_token(lambda k: o_t[:, P * k:P * (k + 1)], now)
                elif name == "att_t":
                    turn_read(now, ("group_out", args[0], GROUPS - 1))
                    by_token(lambda k: att[:, k, :], now)
                elif name == "project":
                    layer = args[0]
                    turn_read(now, ("att_t", layer))
                    buf, _, free = score_of(now)
                    pe.wait_ge(score_free, free)
                    width = OUTC if layer else D
                    w_out = wt[:, WO, KEPT:] if layer else wproj[:, :]
                    for k in range(BLOCKS):
                        ins = nc.tensor.matmul(score[buf][:, width * k:width * (k + 1)], att_t[:, P * k:P * (k + 1)], w_out,
                                               start=True, stop=True)
                    ins.then_inc(score_full, 1)
                elif name == "router":
                    turn_read(now, ("norm_t", 2))
                    for k in range(BLOCKS):
                        ins = nc.tensor.matmul(turn[:, EXPERTS * k:EXPERTS * (k + 1)], n_t[2][:, P * k:P * (k + 1)], gate_t[:, :],
                                               start=True, stop=True)
                    ins.then_inc(turn_full, 1)
                elif name == "expert":
                    u = args[0]
                    at, halves, src = EXPERT_IN[u]
                    if u in EXPERT_NEEDS:
                        written(now, ("expert", EXPERT_NEEDS[u]))
                    srcs = {None: lambda: [n_t[2][:, :]], "h_e3d": lambda: [h_e3d[:, :]]}.get(
                        src, lambda: [hid[src][:, k, :] for k in range(2)])()
                    buf = wide_wait(now)
                    for a in range(halves):
                        for k, moving in enumerate(srcs):
                            ins = nc.tensor.matmul(wide[buf][:, a, :], wt[:, at + len(srcs) * a + k, :], moving,
                                                   start=(k == 0), stop=(k == len(srcs) - 1))
                    ins.then_inc(wide_full, 1)
                elif name == "down":
                    k = args[0]
                    if k == 0:
                        written(now, ("expert", 6))
                        written(now, ("expert", 7))
                    buf, _, free = score_of(now)
                    pe.wait_ge(score_free, free)
                    for e, (at, source) in enumerate(((E0_DN, "h_e0"), (E1_DN, "h_e1"), (E2_DN, "h_l3"), (E3_DN, "h_e3"))):
                        for a in range(2):
                            ins = nc.tensor.matmul(score[buf][:, OUTC * e:OUTC * (e + 1)], hid[source][:, a, P * k:P * (k + 1)],
                                                   wt[:, at + a, KEPT:], start=(a == 0), stop=(a == 1))
                    ins.then_inc(score_full, 1)

            walk(pe, part)


_INS = ['L0_attn_z', 'L0_attn_ln_scale', 'L0_attn_ln_bias', 'L0_attn_w_qkv', 'L0_attn_w_proj', 'L0_attn_b_proj', 'L0_ffn_n1_w',
        'L0_ffn_n2_w', 'L0_ffn_wq', 'L0_ffn_wk', 'L0_ffn_wv', 'L0_ffn_wo', 'L0_ffn_qn_w', 'L0_ffn_kn_w', 'L0_ffn_gate_w',
        'L0_ffn_e0_up', 'L0_ffn_e0_down', 'L0_ffn_e1_w1', 'L0_ffn_e1_w2', 'L0_ffn_e1_down', 'L0_ffn_e2_l1', 'L0_ffn_e2_l2',
        'L0_ffn_e2_l3', 'L0_ffn_e2_l4', 'L0_ffn_e3_down', 'L0_ffn_e3_up', 'L0_ffn_e3_out']


def kernel(**inputs):
    import numpy as _np
    import concourse.bacc as _bacc
    from concourse import mybir as _mybir
    from concourse.bass_utils import run_bass_kernel_spmd as _run

    nc = _bacc.Bacc("TRN2", target_bir_lowering=False, num_devices=1)
    arrays, args = {}, {}
    for name in _INS:
        a = _np.ascontiguousarray(inputs[name])
        arrays[f"in_{name}_dram"] = a
        args[name] = nc.dram_tensor(f"in_{name}_dram", a.shape, _mybir.dt.from_np(a.dtype), kind="ExternalInput").ap()
    result = nc.dram_tensor("out_0_dram", (SEQS, TOKENS, D), F32, kind="ExternalOutput").ap()
    program(nc, args, result)
    r = _run(nc, [arrays], core_ids=[0])
    return r.results[0]["out_0_dram"]
```

```python
from contextlib import ExitStack

import concourse.bass as bass
from concourse import mybir

ALU = mybir.AluOpType
ACT = mybir.ActivationFunctionType
F32 = mybir.dt.float32
BF16 = mybir.dt.bfloat16
U32 = mybir.dt.uint32
AX = mybir.AxisListType

P = 128
SEQS, TOKENS, D = 8, 512, 128
HEADS, HD = 16, 8
BLOCKS = TOKENS // P
GROUP = 4
GROUPS = HEADS // GROUP
ROWS = 64
PAIRS = HEADS // 2
PARTS = 6
MAX_ROW = PARTS * HD
KEPT = 32
OUTC = D - KEPT
EXPERTS = 4
STEPS = GROUPS * BLOCKS
TILES = HEADS * BLOCKS
GTILES = TILES // GROUPS
AHEAD = 22
LAG = 2
RING = 4
SOON = 30
SHARES = (2, 3, 1, 0)
TILES2 = '7444 6223 1002 4063'
TILES1 = '6246 2343 3363 8768'
BESIDE2 = (
    (1, "preparation 1", "stats", 0),
    (3, "preparation 1", "apply", 0),
    (3, "preparation 1", "stats", 1),
    (5, "attention 2", "keep_y"),
    (5, "end of attention 1", "group_out", 0, 3),
    (6, "preparation 1", "apply", 1),
    (7, "end of attention 1", "att_t", 0),
    (8, "preparation 1", "norm_t", 0),
    (9, "end of attention 1", "project", 0),
    (9, "preparation 1", "qk", 0),
    (9, "end of attention 1", "stats", 2),
    (11, "preparation 1", "part1", 0),
    (11, "end of attention 1", "apply", 2),
    (11, "end of attention 1", "stats", 3),
    (12, "preparation 1", "v", 0),
    (12, "preparation 1", "part2", 0),
    (12, "preparation 1", "parts_in_rows", 0),
    (13, "preparation 1", "res1"),
    (14, "end of attention 1", "apply", 3),
    (15, "preparation 1", "rows", 0, "q", 0),
    (17, "preparation 1", "rows", 0, "q", 1),
    (18, "end of attention 1", "norm_t", 1),
    (19, "preparation 1", "rows", 0, "k", 0),
    (21, "preparation 1", "rows", 0, "k", 1),
    (21, "end of attention 1", "qk", 1),
    (23, "end of attention 1", "head_rms", 0),
    (27, "end of attention 1", "head_rms", 1),
    (31, "end of attention 1", "head_rms", 2),
)
BESIDE1 = (
    (3, "preparation 2", "part1", 1),
    (4, "preparation 2", "v", 1),
    (5, "preparation 2", "part2", 1),
    (5, "preparation 2", "parts_in_rows", 1),
    (5, "experts", "group_out", 1, 3),
    (9, "experts", "att_t", 1),
    (11, "experts", "project", 1),
    (11, "experts", "stats", 4),
    (11, "preparation 2", "rows", 1, "q", 0),
    (13, "experts", "apply", 4),
    (13, "preparation 2", "rows", 1, "q", 1),
    (13, "experts", "norm_t", 2),
    (15, "preparation 2", "rows", 1, "k", 0),
    (15, "experts", "router"),
    (15, "experts", "expert", 0),
    (15, "experts", "expert", 1),
    (17, "experts", "route", 0),
    (18, "preparation 2", "rows", 1, "k", 1),
    (19, "experts", "route", 1),
    (19, "experts", "expert", 2),
    (19, "experts", "expert", 3),
    (19, "experts", "expert", 7),
    (21, "experts", "expert", 5),
    (21, "experts", "expert", 4),
    (23, "experts", "expert", 6),
    (25, "experts", "down", 0),
    (29, "experts", "down", 1),
    (29, "experts", "down", 2),
    (29, "experts", "down", 3),
)

SCALE = float(HD) ** -0.5
LN_EPS = 1e-5
RMS_EPS = 1.1920929e-07
MASKED = -1e30
F32_MAX = 3.4028234663852886e38

WQKV2, WO, E0_UP, E1_W1, E1_W2, E2_L1, E3_DOWN, E2_L2, E2_L3, E3_UP, E0_DN, E1_DN, E2_DN, E3_DN = (
    0, 3, 4, 6, 8, 10, 12, 13, 17, 21, 23, 25, 27, 29)
NWT = 31

SETUP_FILLS = {"wide": (NWT + 7) // 8, "score": 2, "turn": 1, "pv": 0, "step": 0}
FILLS = {
    "wide": ("qk", "v", "rows", "shifted", "expert"),
    "score": ("score", "project", "down"),
    "turn": ("norm_t", "max_rows", "group_out", "att_t", "router"),
    "pv": ("values",),
    "step": ("shifted",),
}


def chosen(plan, wanted):
    beside = {i: [] for i in range(2 * STEPS)}
    for i, part, *task in plan:
        beside[i] += [tuple(task)] if wanted[part] else []
    return beside


def attention(layer, earlier, following, scores, tiles, beside):
    order = []
    tiles = [int(n) for n in tiles.replace(" ", "")]
    for i in range(STEPS):
        g, kb = divmod(i, BLOCKS)
        share = [(tiles[i] + k) // 4 for k in SHARES]
        order += scores(share[0])
        if i >= LAG:
            order.append(("values", layer, i - LAG))
        elif earlier is not None:
            order.append(("values", earlier, STEPS - LAG + i))
        order += scores(share[1]) + [("shifted", layer, i, 0)] + beside[2 * i] + scores(share[2])
        if kb == BLOCKS - 1:
            if g < GROUPS - 1:
                order += scores.up_to(layer, GTILES * (g + 2)) + [("max_rows", layer, g + 1)]
            elif following is not None:
                order += scores.up_to(following, GTILES) + [("max_rows", following, 0)]
        order += [("shifted", layer, i, 1)] + scores(share[3])
        if kb == LAG and g > 0:
            order.append(("group_out", layer, g - 1))
        order += beside[2 * i + 1]
    return order


def alone(beside, following, tiles):
    tasks = [task for names in beside.values() for task in names]
    if not tiles:
        return tasks
    ready = tasks.index(("rows", following, "k", 1)) + 1
    order = tasks[:ready]
    scores = Scores(tiles)
    for task in tasks[ready:]:
        order += scores(2) + [task]
    return order + scores(TILES) + [("max_rows", following, 0)]


class Scores:

    def __init__(self, tiles):
        self.tiles = list(tiles)

    def __call__(self, n):
        out, self.tiles = self.tiles[:n], self.tiles[n:]
        return out

    def up_to(self, layer, n):
        return self(1 + max((i for i, task in enumerate(self.tiles) if task[1] == layer and task[2] < n), default=-1))


def tiles_of(layer, start, stop):
    return [("score", layer, n) for n in range(start, stop)]


def last_values(layer):
    return [("values", layer, i) for i in range(STEPS - LAG, STEPS)]


def first_half(att2, att1_ends, pro1):
    beside = chosen(BESIDE2, {"attention 2": att2, "end of attention 1": att1_ends, "preparation 1": pro1})
    late = tiles_of(0, 0, AHEAD) if pro1 else []
    if not att2:
        return (last_values(0) if att1_ends else []) + alone(beside, 0, late)
    scores = Scores(tiles_of(1, SOON, TILES) + late)
    order = attention(1, 0 if att1_ends else None, 0 if pro1 else None, scores, TILES2, beside) + scores(TILES)
    return order + ([] if pro1 else last_values(1))


def second_half(att1, ffn, pro2):
    beside = chosen(BESIDE1, {"preparation 2": pro2, "experts": ffn})
    soon = tiles_of(1, 0, SOON) if pro2 else []
    if not att1:
        return alone(beside, 1, soon)
    scores = Scores(tiles_of(0, AHEAD, TILES) + soon)
    return attention(0, 1 if ffn else None, 1 if pro2 else None, scores, TILES1, beside) + scores(TILES)


class Slot:

    def __init__(self, times, order, before, earlier):
        self.times, self.order, self.earlier = times, order, earlier
        self.base, self.per, self.index = dict(before), {}, {}
        for name, kinds in FILLS.items():
            fills = [n for n, task in enumerate(order) if task[0] in kinds]
            self.index[name] = {n: i for i, n in enumerate(fills)}
            self.per[name] = len(fills)
        self.done = {}
        assert times == 1 or all(self.per[n] % 2 == 0 for n in ("wide", "score"))

    def after(self):
        return {n: self.base[n] + self.times * self.per[n] for n in FILLS}

    def place(self, name, at, task):
        found = [n for n in range(at + 1) if self.order[n] == task]
        if found:
            return self.base[name] + self.index[name][found[-1]], self.per[name]
        first, per = self.earlier.place(name, len(self.earlier.order) - 1, task)
        first += (self.earlier.times - 1) * per
        if self.times > 1:
            own = self.base[name] - self.per[name] + self.index[name][self.order.index(task)]
            assert own == first, (name, task, own, first)
        return first, self.per[name]


def slots():
    start = ([("stats", 0), ("apply", 0), ("stats", 1), ("apply", 1), ("norm_t", 0), ("qk", 0), ("v", 0), ("part1", 0),
              ("part2", 0), ("parts_in_rows", 0), ("res1",), ("rows", 0, "q", 0), ("rows", 0, "q", 1), ("rows", 0, "k", 0),
              ("rows", 0, "k", 1)] + tiles_of(0, 0, AHEAD) + [("max_rows", 0, 0)])
    out, before, done = [], SETUP_FILLS, {}
    for times, order in (
            (1, start + second_half(True, False, False)),
            (1, first_half(False, True, True) + second_half(True, False, True)),
            (SEQS - 2, first_half(True, True, True) + second_half(True, True, True)),
            (1, first_half(True, True, False) + second_half(False, True, True)),
            (1, first_half(True, False, False) + second_half(False, True, False))):
        slot = Slot(times, order, before, out[-1] if out else None)
        slot.done = {**{task: 0 for task in order}, **done}
        for task in order:
            done[task] = done.get(task, 0) + times
        out.append(slot)
        before = slot.after()
    assert all(n == SEQS for n in done.values()), done
    return out


SLOTS = slots()


class Now:

    def __init__(self, slot, j=None):
        self.slot, self.j, self.n = slot, j, 0

    def count(self, value, per):
        return value if self.j is None else self.j * per + value

    def seq(self, per=1, c=0):
        return self.count(self.slot.done.get(self.slot.order[self.n], 0) * per + c, per)

    def first_seq(self):
        return self.j is None and self.slot.done.get(self.slot.order[self.n], 0) == 0

    def fill(self, name, task=None):
        return self.slot.place(name, self.n, self.slot.order[self.n] if task is None else task)


def walk(engine, part):
    for slot in SLOTS:
        if slot.times == 1:
            now = Now(slot)
            for now.n, task in enumerate(slot.order):
                part(now, *task)
        else:
            with engine.Fori(0, slot.times) as j:
                now = Now(slot, j)
                for now.n, task in enumerate(slot.order):
                    part(now, *task)


def program(nc, t, out):
    with ExitStack() as ctx:
        def sb(name, shape, dt=F32):
            return ctx.enter_context(nc.sbuf_tensor(name, shape, dt))

        def psum(name, shape, dt=F32):
            return ctx.enter_context(nc.psum_tensor(name, shape, dt))

        def sem(name):
            return ctx.enter_context(nc.semaphore(name))

        room = sb("room", [P, 5 * 2 * TOKENS])
        stage = room[:, 0:NWT * P].rearrange("p (a n) -> p a n", n=P)
        wqkv_raw = room[:, NWT * P:NWT * P + 3 * D]
        spare = room[:, NWT * P + 3 * D:]
        mask_f = spare[:, 0:2 * P].rearrange("p (a n) -> p a n", a=2)
        gate_raw = spare[0:EXPERTS, 2 * P:3 * P]
        ones_row = spare[0:1, 3 * P:4 * P]
        row = spare[0:1, 4 * P:4 * P + D + 2 * HD]
        hid = {name: room[:, 2 * TOKENS * i:2 * TOKENS * (i + 1)].rearrange("p (a n) -> p a n", a=2)
               for i, name in enumerate(("h_e1", "h_l1", "h_l2", "h_e3", "h_e0"))}
        hid["h_l3"] = hid["h_l1"]
        h_e3d = sb("h_e3d", [P, TOKENS])
        wt = sb("wt", [P, NWT, P])
        wqkv1 = sb("wqkv1", [P, 3, D])
        wproj = sb("wproj", [P, D])
        gate_t = sb("gate_t", [P, EXPERTS])
        b_proj = sb("b_proj", [P, D])
        qk_w = sb("qk_w", [P, 2, HD])
        cols = sb("cols", [P, 4])
        id_f = sb("id_f", [P, P])
        id_b = sb("id_b", [P, P], BF16)
        mask_qk = sb("mask_qk", [P, P], BF16)
        mask_kq = sb("mask_kq", [P, P], BF16)
        before = sb("before", [P, EXPERTS, EXPERTS])
        behind = sb("behind", [P, EXPERTS, EXPERTS])
        eps = sb("eps", [P, 3, BLOCKS])
        credit = sb("credit", [P, 4])

        def token_tile(name):
            return sb(name, [P, BLOCKS, D])

        x, z, res1 = token_tile("x"), token_tile("z"), token_tile("res1")
        x1_new, y_new = token_tile("x1_new"), token_tile("y_new")
        x1, y = token_tile("x1"), token_tile("y")
        att = token_tile("att")
        att_t = sb("att_t", [P, TOKENS])
        n = [token_tile(f"n{i}") for i in range(2)]
        n.append(n[0])
        n_t = [sb(f"n_t{i}", [P, TOKENS]) for i in range(2)] + [att_t]
        bn = [sb(f"bn{i}", [P, BLOCKS, 6]) for i in range(5)]
        mv = [sb(f"mv{i}", [P, BLOCKS, 2]) for i in range(5)]
        ms = [sb(f"ms{i}", [P, BLOCKS]) for i in range(5)]
        ms2 = [sb(f"msq{i}", [P, BLOCKS]) for i in range(5)]
        rstd = [sb(f"rstd{i}", [P, BLOCKS]) for i in range(5)]
        qk = sb("qk", [P, 2, BLOCKS, D])
        rest = sb("rest", [P, 2, BLOCKS, D])
        hsum = sb("hsum", [P, 2 * BLOCKS * HEADS])
        hstep = sb("hstep", [P, 2 * BLOCKS * HEADS])
        hrstd = sb("hrstd", [P, 2 * BLOCKS * HEADS])
        part1 = sb("part1", [P, 2, BLOCKS, D], BF16)
        part2 = sb("part2", [P, 2, BLOCKS, D], BF16)
        q_tok = [sb(f"q_tok{i}", [P, BLOCKS, HEADS, ROWS], BF16) for i in range(2)]
        k_tok = sb("k_tok", [P, BLOCKS, HEADS, ROWS], BF16)
        q_t = [sb(f"q_t{i}", [P, PAIRS, TOKENS], BF16) for i in range(2)]
        k_t = [sb(f"k_t{i}", [P, 2, PAIRS, TOKENS], BF16) for i in range(2)]
        v_one = [sb(f"v_one{i}", [P, BLOCKS, HEADS, 32]) for i in range(2)]
        neg_max = sb("neg_max", [P, 2, BLOCKS, HEADS])
        probs = sb("probs", [P, RING, GROUP, TOKENS])
        o_t = sb("o_t", [P, TOKENS])
        rec = sb("rec", [P, BLOCKS, GROUP])
        lg = sb("lg", [P, BLOCKS, EXPERTS])
        lg_ok = sb("lg_ok", [P, BLOCKS, EXPERTS], U32)
        lgc = sb("lgc", [P, BLOCKS, EXPERTS])
        lmax = sb("lmax", [P, BLOCKS])
        lexp = sb("lexp", [P, BLOCKS, EXPERTS])
        prob = sb("prob", [P, BLOCKS, EXPERTS])
        ahead = sb("ahead", [P, BLOCKS, EXPERTS, EXPERTS])
        ahead2 = sb("ahead2", [P, BLOCKS, EXPERTS, EXPERTS])
        rank = sb("rank", [P, BLOCKS, EXPERTS])
        wts = sb("wts", [P, BLOCKS, EXPERTS])

        wide = [psum(f"wide{i}", [P, 2, 512]) for i in range(2)]
        score = [psum(f"score{i}", [P, 512]) for i in range(2)]
        pv = psum("pv", [P, 512])
        turn = psum("turn", [P, 512])
        turn_tok = turn[:, :].rearrange("p (t c) -> p t c", t=BLOCKS)

        w_loaded = sem("w_loaded")
        x_loaded = sem("x_loaded")
        out_stored = sem("out_stored")
        consts = sem("consts")
        w_ready = sem("w_ready")
        wide_full = sem("wide_full")
        wide_free = [sem(f"wide_free{i}") for i in range(2)]
        score_full = sem("score_full")
        score_free = sem("score_free")
        turn_full = sem("turn_full")
        turn_free = sem("turn_free")
        pv_done = sem("pv_done")
        ot_ready = sem("ot_ready")
        pool_step = sem("pool_step")
        stats_ready = [sem(f"stats_ready{i}") for i in range(5)]
        rstd_ready = [sem(f"rstd_ready{i}") for i in range(5)]
        n_ready = [sem(f"n_ready{i}") for i in range(3)]
        nt_ready = [sem(f"nt_ready{i}") for i in range(3)]
        res1_ready = sem("res1_ready")
        y_ready = sem("y_ready")
        kept = sem("kept")
        u_ready = sem("u_ready")
        sum_ready = sem("sum_ready")
        parts_ready = [sem(f"parts_ready{i}") for i in range(2)]
        q3_ready = [sem(f"q3_ready{i}") for i in range(2)]
        qtok_ready = [sem(f"qtok_ready{i}") for i in range(2)]
        ktok_ready = [sem(f"ktok_ready{i}") for i in range(2)]
        k_even = [sem(f"k_even{i}") for i in range(2)]
        max_ready = [sem(f"max_ready{i}") for i in range(2)]
        qmax_ready = [sem(f"qmax_ready{i}") for i in range(2)]
        att_t_ready = [sem(f"att_t_ready{i}") for i in range(2)]
        logits_ready = sem("logits_ready")
        lexp_ready = sem("lexp_ready")

        def wide_of(now, task=None):
            first, per = now.fill("wide", task)
            return first % 2, now.count(first + 1, per), now.count(first // 2, per // 2), now.count(first // 2 + 1, per // 2)

        def score_of(now):
            first, per = now.fill("score")
            return first % 2, now.count(first + 1, per), now.count(first - 1, per)

        def turn_of(now):
            first, per = now.fill("turn")
            return now.count(first + 1, per), now.count(first, per)

        def step_of(now, layer, i):
            return now.fill("pv", ("values", layer, i))

        def flat(a):
            return a.rearrange("p a n -> p (a n)")

        W_LOADS = 26
        W_SETUP = SETUP_FILLS["wide"]
        block = ctx.enter_context(nc.Block())

        @block.sync
        def _(sp):
            def load(dst, src):
                sp.dma_start(dst, src).then_inc(w_loaded, 16)

            DOWN = ("down", BLOCKS - 1)

            def store(s):
                slot = next(a for a in SLOTS if a.done.get(DOWN, 0) <= s < a.done.get(DOWN, 0) + a.times * a.order.count(DOWN))
                last = slot.place("score", len(slot.order) - 1, DOWN)[0] + (s - slot.done[DOWN]) * slot.per["score"]
                sp.wait_ge(score_free, last + 1)
                sp.dma_start(dst[s], x1[:, :, :]).then_inc(out_stored, 16)

            load(wqkv_raw, t["L0_attn_w_qkv"])
            for i, name in enumerate(("ln_scale", "ln_bias")):
                load(cols[:, i:i + 1], t[f"L0_attn_{name}"].rearrange("(p a) -> p a", a=1))
            for i, name in enumerate(("n1_w", "n2_w")):
                load(cols[:, 2 + i:3 + i], t[f"L0_ffn_{name}"].rearrange("(p a) -> p a", a=1))
            load(row[:, 0:D], t["L0_attn_b_proj"].rearrange("(a n) -> a n", a=1))
            load(row[:, D:D + HD], t["L0_ffn_qn_w"].rearrange("(a n) -> a n", a=1))
            load(row[:, D + HD:], t["L0_ffn_kn_w"].rearrange("(a n) -> a n", a=1))
            load(wproj[:, :], t["L0_attn_w_proj"])
            load(gate_raw[:, :], t["L0_ffn_gate_w"])
            for i, name in enumerate(("wq", "wk", "wv", "wo")):
                load(stage[:, i, :], t[f"L0_ffn_{name}"])
            load(stage[:, E3_DOWN, :], t["L0_ffn_e3_down"])
            for at, name in ((E0_UP, "e0_up"), (E1_W1, "e1_w1"), (E1_W2, "e1_w2"), (E2_L1, "e2_l1"), (E3_UP, "e3_up")):
                sp.dma_start(stage[:, at:at + 2, :], t[f"L0_ffn_{name}"].rearrange("(a p) c -> p a c", p=P)).then_inc(w_loaded, 16)
            for at, name in ((E2_L2, "e2_l2"), (E2_L3, "e2_l3")):
                sp.dma_start(stage[:, at:at + 4, :].rearrange("p (a k) c -> p a (k c)", a=2),
                             t[f"L0_ffn_{name}"].rearrange("(a p) n -> p a n", p=P)).then_inc(w_loaded, 16)
            for at, name in ((E0_DN, "e0_down"), (E1_DN, "e1_down"), (E2_DN, "e2_l4"), (E3_DN, "e3_out")):
                load(stage[:, at:at + 2, :].rearrange("p k c -> p (k c)"), t[f"L0_ffn_{name}"])
            src = t["L0_attn_z"].rearrange("b (t p) d -> b p t d", p=P)
            dst = out.rearrange("b (t p) d -> b p t d", p=P)
            sp.dma_start(x[:, :, :], src[0]).then_inc(x_loaded, 16)
            for s in range(SEQS):
                if s + 1 < SEQS:
                    sp.wait_ge(res1_ready, s + 1)
                    sp.dma_start(x[:, :, :], src[s + 1]).then_inc(x_loaded, 16)
                if s > 1:
                    store(s - 2)
            store(SEQS - 2)
            store(SEQS - 1)
            sp.wait_ge(out_stored, 16 * (SEQS + 1))
        @block.gpsimd
        def _(pool):
            steps = [0]

            def link(ins):
                steps[0] += 1
                ins.then_inc(pool_step, 1)
                pool.wait_ge(pool_step, steps[0])

            nc.gpsimd.memset(id_f[:, :], 0.0)
            nc.gpsimd.memset(mask_f[:, :, :], 0.0)
            nc.gpsimd.memset(before[:, :, :], 1.0)
            for i, value in enumerate((LN_EPS, RMS_EPS, -0.5)):
                nc.gpsimd.memset(eps[:, i, :], value)
            nc.gpsimd.memset(behind[:, :, :], 1.0)
            link(nc.gpsimd.memset(ones_row[:, :], 1.0))
            nc.gpsimd.affine_select(out=id_f[:, :], in_=id_f[:, :], compare_op=ALU.not_equal, fill=1.0,
                                    base=0, pattern=[[-1, P]], channel_multiplier=1)
            nc.gpsimd.affine_select(out=mask_f[:, 0, :], in_=mask_f[:, 0, :], compare_op=ALU.is_ge, fill=MASKED,
                                    base=0, pattern=[[-1, P]], channel_multiplier=1)
            nc.gpsimd.affine_select(out=mask_f[:, 1, :], in_=mask_f[:, 1, :], compare_op=ALU.is_ge, fill=MASKED,
                                    base=0, pattern=[[1, P]], channel_multiplier=-1)
            nc.gpsimd.affine_select(out=before[:, :, :], in_=before[:, :, :], compare_op=ALU.is_gt, fill=0.0,
                                    base=0, pattern=[[1, EXPERTS], [-1, EXPERTS]], channel_multiplier=0)
            link(nc.gpsimd.affine_select(out=behind[:, :, :], in_=behind[:, :, :], compare_op=ALU.is_gt, fill=0.0,
                                         base=0, pattern=[[-1, EXPERTS], [1, EXPERTS]], channel_multiplier=0))
            nc.gpsimd.tensor_copy(id_b[:, :], id_f[:, :])
            nc.gpsimd.tensor_copy(mask_qk[:, :], mask_f[:, 0, :])
            nc.gpsimd.tensor_copy(mask_kq[:, :], mask_f[:, 1, :]).then_inc(consts, 1)
            for i in range(2):
                nc.gpsimd.memset(q_tok[i][:, :, :, :], 0.0)
                nc.gpsimd.memset(k_t[i][:, :, :, :], 0.0)
                nc.gpsimd.memset(v_one[i][:, :, :, :], 0.0)
            link(nc.gpsimd.memset(k_tok[:, :, :, :], 0.0))
            for i in range(2):
                nc.gpsimd.memset(v_one[i][:, :, :, HD:HD + 1], 1.0)
            nc.gpsimd.memset(k_tok[:, :, :, MAX_ROW:MAX_ROW + 2], 1.0).then_inc(consts, 1)
            nc.gpsimd.memset(credit[:, 1:2], 0.0).then_inc(out_stored, 16)
            pool.wait_ge(w_ready, 3)

            def add(out, a, b):
                return nc.gpsimd.tensor_tensor(out, a, b, ALU.add)

            def part(now, name, *args):
                if name == "stats":
                    w = args[0]
                    pool.wait_ge(stats_ready[w], now.seq(1, 1))
                    if w >= 3:
                        nc.gpsimd.tensor_tensor(ms2[w][:, :], mv[w][:, :, 0], mv[w][:, :, 0], ALU.mult)
                        pool.drain()
                        add(ms2[w][:, :], ms2[w][:, :], mv[w][:, :, 1])
                        pool.drain()
                        add(ms[w][:, :], ms2[w][:, :], eps[:, 1, :])
                    else:
                        add(ms[w][:, :], mv[w][:, :, 1], eps[:, 0, :])
                    pool.drain()
                    nc.gpsimd.tensor_tensor(rstd[w][:, :], ms[w][:, :], eps[:, 2, :], ALU.pow).then_inc(rstd_ready[w], 1)
                elif name == "res1":
                    pool.wait_ge(n_ready[0], now.seq(1, 1))
                    add(res1[:, :, :], x[:, :, :], z[:, :, :])
                    pool.drain()
                    add(res1[:, :, :], res1[:, :, :], b_proj[:, :].unsqueeze(1).broadcast_to([P, BLOCKS, D])).then_inc(res1_ready, 1)
                elif name == "keep_y":
                    pool.wait_ge(out_stored, now.seq(16, 16))
                    pool.wait_ge(y_ready, now.seq(1, 1))
                    add(credit[:, 3:4], eps[:, 0, 0:1], eps[:, 0, 0:1])
                    nc.gpsimd.tensor_copy(x1[:, :, :], x1_new[:, :, :])
                    nc.gpsimd.tensor_copy(y[:, :, :], y_new[:, :, :]).then_inc(kept, 1)
                elif name == "parts_in_rows":
                    layer = args[0]
                    k_rows = k_tok[:, :, :, :].rearrange("p t h r -> p (t h) r")[:, :, 0:MAX_ROW].rearrange(
                        "p g (s d) -> p g s d", d=HD)
                    p1, p2, r = (a[:, 1, :, :].rearrange("p t (h d) -> p (t h) d", d=HD) for a in (part1, part2, rest))
                    G = BLOCKS * HEADS
                    pool.wait_ge(parts_ready[layer], now.seq(2, 2))
                    nc.gpsimd.tensor_tensor(k_rows[:, :, 5, :], r, p2, ALU.subtract)
                    nc.gpsimd.tensor_copy(k_rows[:, :, 0:5:2, :], p1.unsqueeze(2).broadcast_to([P, G, 3, HD]))
                    nc.gpsimd.tensor_copy(k_rows[:, :, 1:4:2, :], p2.unsqueeze(2).broadcast_to([P, G, 2, HD])).then_inc(ktok_ready[layer], 1)
                elif name == "project" and args[0] == 1:
                    pool.wait_ge(u_ready, now.seq(1, 1))
                    add(x1[:, :, :], x1[:, :, :], y[:, :, :]).then_inc(sum_ready, 1)

            walk(pool, part)

        @block.scalar
        def _(act):
            act.wait_ge(w_loaded, 16 * W_LOADS)
            raw = wqkv_raw.rearrange("p (n j) -> p j n", j=3)
            nc.scalar.activation(wqkv1[:, 0, :], raw[:, 0, :], ACT.Copy, scale=SCALE)
            nc.scalar.activation(wqkv1[:, 1:3, :], raw[:, 1:3, :], ACT.Copy).then_inc(w_ready, 1)
            for u in range(0, W_SETUP, 2):
                act.wait_ge(wide_full, u + 1)
                nc.scalar.activation(wt[:, 8 * u:8 * u + 8, :].rearrange("p (a c) n -> p a (c n)", a=2),
                                     wide[0][:, :, :], ACT.Copy).then_inc(wide_free[0], 1)

            HIDDEN = (("h_e1", ACT.Silu), None, ("h_l1", ACT.Gelu), ("h_e3d", ACT.Gelu), ("h_l2", ACT.Gelu),
                      ("h_e3", ACT.Gelu), ("h_l3", ACT.Gelu), ("h_e0", ACT.Gelu))

            def part(now, name, *args):
                if name == "norm_t":
                    w = args[0]
                    act.wait_ge(turn_full, turn_of(now)[0])
                    if w == 0:
                        ins = nc.scalar.activation(n_t[0][:, :], turn[:, :], ACT.Identity, scale=cols[:, 0:1], bias=cols[:, 1:2])
                    else:
                        ins = nc.scalar.activation(n_t[w][:, :], turn[:, :], ACT.Copy, scale=cols[:, w + 1:w + 2])
                    ins.then_inc(turn_free, 1)
                elif name == "qk":
                    layer = args[0]
                    buf, full, _, _ = wide_of(now)
                    act.wait_ge(wide_full, full)
                    nc.scalar.activation(qk[:, :, :, :], flat(wide[buf][:, :, :]).rearrange("p (t a n) -> p a t n", a=2, n=D),
                                         ACT.Copy).then_inc(wide_free[buf], 1)
                elif name == "v":
                    layer = args[0]
                    buf, full, _, _ = wide_of(now)
                    act.wait_ge(wide_full, full)
                    nc.scalar.activation(v_one[layer][:, :, :, 0:HD], wide[buf][:, 0, :].rearrange("p (t h d) -> p t h d", h=HEADS, d=HD),
                                         ACT.Copy).then_inc(wide_free[buf], 1)
                elif name == "parts_in_rows":
                    layer = args[0]
                    q_rows = q_tok[layer][:, :, :, :].rearrange("p t h r -> p (t h) r")[:, :, 0:MAX_ROW].rearrange(
                        "p g (s d) -> p g s d", d=HD)
                    p1, p2 = (a[:, 0, :, :].rearrange("p t (h d) -> p (t h) d", d=HD) for a in (part1, part2))
                    G = BLOCKS * HEADS
                    act.wait_ge(parts_ready[layer], now.seq(2, 2))
                    nc.scalar.activation(q_rows[:, :, 0:2, :], p1.unsqueeze(2).broadcast_to([P, G, 2, HD]), ACT.Copy)
                    nc.scalar.activation(q_rows[:, :, 5, :], p1, ACT.Copy)
                    nc.scalar.activation(q_rows[:, :, 2:4, :], p2.unsqueeze(2).broadcast_to([P, G, 2, HD]), ACT.Copy).then_inc(qtok_ready[layer], 1)
                elif name == "rows":
                    layer, what, half = args
                    if what == "k":
                        buf, full, _, _ = wide_of(now)
                        act.wait_ge(wide_full, full)
                        nc.scalar.activation(flat(k_t[layer][0:ROWS, 0, 4 * half:4 * half + 4, :]),
                                             flat(wide[buf][0:ROWS, :, :]).bitcast(BF16), ACT.Copy).then_inc(k_even[layer], 1)
                elif name == "max_rows":
                    layer, g = args
                    act.wait_ge(turn_full, turn_of(now)[0])
                    nc.scalar.activation(flat(q_t[layer][:, 2 * g:2 * g + 2, :]), turn[:, :].bitcast(BF16), ACT.Copy).then_inc(turn_free, 1)
                elif name == "shifted":
                    layer, i, half = args
                    buf, full, _, _ = wide_of(now)
                    first, per = (c // 2 for c in now.fill("step"))
                    if half == 0 and first >= RING:
                        act.wait_ge(pv_done, now.count(first - RING + 1, per))
                    act.wait_ge(wide_full, full)
                    c0 = P * (i % BLOCKS) if layer else 0
                    nc.scalar.activation(probs[:, i % RING, 2 * half:2 * half + 2, c0:], wide[buf][:, :, c0:],
                                         ACT.Exp).then_inc(wide_free[buf], 1)
                elif name == "values" and args[1] % BLOCKS == BLOCKS - 1:
                    first, per = step_of(now, *args)
                    act.wait_ge(pv_done, now.count(first + 1, per))
                    nc.scalar.activation(o_t[:, :], pv[:, :], ACT.Copy).then_inc(ot_ready, 1)
                elif name == "att_t":
                    act.wait_ge(turn_full, turn_of(now)[0])
                    nc.scalar.activation(att_t[:, :], turn[:, :], ACT.Copy).then_inc(turn_free, 1)
                elif name == "route" and args[0] == 0:
                    act.wait_ge(logits_ready, now.seq(1, 1))
                    nc.scalar.activation(lexp[:, :, :], lgc[:, :, :], ACT.Exp).then_inc(lexp_ready, 1)
                elif name == "expert" and HIDDEN[args[0]]:
                    target, fn = HIDDEN[args[0]]
                    buf, full, _, _ = wide_of(now)
                    act.wait_ge(wide_full, full)
                    if target == "h_e3d":
                        ins = nc.scalar.activation(h_e3d[:, :], wide[buf][:, 0, :], fn)
                    else:
                        ins = nc.scalar.activation(hid[target], wide[buf][:, :, :], fn)
                    ins.then_inc(wide_free[buf], 1)

            walk(act, part)

        @block.vector
        def _(dve):
            nc.vector.memset(credit[:, 0:1], 0.0).then_inc(score_free, 2)
            nc.vector.memset(credit[:, 2:3], 0.0).then_inc(score_full, 2)
            for u in range(1, W_SETUP, 2):
                dve.wait_ge(wide_full, u + 1)
                m = min(8, NWT - 8 * u)
                nc.vector.tensor_copy(wt[:, 8 * u:8 * u + m, :].rearrange("p a n -> p (a n)"),
                                      wide[1][:, :, :].rearrange("p a n -> p (a n)")[:, 0:m * P]).then_inc(wide_free[1], 1)
            dve.wait_ge(turn_full, 1)
            nc.vector.tensor_copy(gate_t[:, :], turn[:, 0:EXPERTS])
            nc.vector.tensor_copy(b_proj[:, :], turn[:, 128:256]).then_inc(w_ready, 1)
            rows = turn[:, 256:256 + 2 * HD].rearrange("p (a d) -> p a d", a=2)
            nc.vector.tensor_copy(qk_w[:, 1, :], rows[:, 1, :])
            nc.vector.tensor_scalar(qk_w[:, 0, :], rows[:, 0, :], SCALE, None, ALU.mult).then_inc(turn_free, 1)
            nc.vector.memset(lgc[:, :, :], 0.0).then_inc(w_ready, 1)

            def settle():
                dve.drain()

            def qk_written(now, layer):
                buf, _, _, used = wide_of(now, ("qk", layer))
                dve.wait_ge(wide_free[buf], used)

            def part(now, name, *args):
                if name == "stats":
                    w = args[0]
                    settle()
                    if w == 0:
                        dve.wait_ge(x_loaded, now.seq(16, 16))
                    for k in range(BLOCKS):
                        nc.vector.bn_stats(bn[w][:, k, :], NORM[w][0][:, k, :])
                    settle()
                    for k in range(BLOCKS):
                        ins = nc.vector.bn_aggr(mv[w][:, k, :], bn[w][:, k, :])
                    ins.then_inc(stats_ready[w], 1)
                elif name == "apply":
                    w = args[0]
                    src, dst = NORM[w]
                    dve.wait_ge(rstd_ready[w], now.seq(1, 1))
                    for k in range(BLOCKS):
                        if w < 3:
                            ins = nc.vector.tensor_scalar(dst[:, k, :], src[:, k, :], mv[w][:, k, 0:1], rstd[w][:, k:k + 1],
                                                          ALU.subtract, ALU.mult)
                        else:
                            ins = nc.vector.tensor_scalar(dst[:, k, :], src[:, k, :], rstd[w][:, k:k + 1], None, ALU.mult)
                    if w > 0:
                        ins.then_inc({1: n_ready[0], 2: y_ready, 3: n_ready[1], 4: n_ready[2]}[w], 1)
                elif name == "head_rms":
                    qk_all = qk[:, :, :, :].rearrange("p a t n -> p (a t n)")
                    heads = qk_all.rearrange("p (g d) -> p g d", d=HD)
                    if args[0] == 0:
                        qk_written(now, 1)
                        sq = rest[:, :, :, :].rearrange("p a t n -> p (a t n)")
                        nc.vector.tensor_tensor(sq, qk_all, qk_all, ALU.mult)
                        settle()
                        nc.vector.tensor_reduce(hsum[:, :], sq.rearrange("p (g d) -> p g d", d=HD), AX.X, ALU.add)
                        settle()
                        nc.vector.tensor_scalar(hsum[:, :], hsum[:, :], 1.0 / HD, RMS_EPS, ALU.mult, ALU.add)
                    elif args[0] == 1:
                        nc.vector.tensor_scalar(hrstd[:, :].bitcast(U32), hsum[:, :].bitcast(U32), -0.5, 1597463007.0, ALU.mult, ALU.add)
                        settle()
                        for _ in range(3):
                            nc.vector.scalar_tensor_tensor(out=hstep[:, :], in0=hsum[:, :], scalar=-0.5, in1=hrstd[:, :],
                                                           op0=ALU.mult, op1=ALU.mult)
                            settle()
                            nc.vector.tensor_tensor(hstep[:, :], hstep[:, :], hrstd[:, :], ALU.mult)
                            settle()
                            nc.vector.scalar_tensor_tensor(out=hrstd[:, :], in0=hstep[:, :], scalar=1.5, in1=hrstd[:, :],
                                                           op0=ALU.add, op1=ALU.mult)
                            settle()
                    else:
                        nc.vector.tensor_tensor(heads, heads, hrstd[:, :].unsqueeze(2).broadcast_to([P, 2 * BLOCKS * HEADS, HD]), ALU.mult)
                        settle()
                        both = qk_all.rearrange("p (a g d) -> p a g d", a=2, d=HD)
                        nc.vector.tensor_tensor(both, both, qk_w[:, :, :].unsqueeze(2).broadcast_to([P, 2, BLOCKS * HEADS, HD]), ALU.mult)
                    settle()
                elif name == "part1":
                    layer = args[0]
                    qk_written(now, layer)
                    f1, qk_all, r = (a[:, :, :, :].rearrange("p a t n -> p (a t n)") for a in (part1, qk, rest))
                    nc.vector.tensor_copy(f1, qk_all)
                    settle()
                    nc.vector.tensor_tensor(r, qk_all, f1, ALU.subtract).then_inc(parts_ready[layer], 1)
                elif name == "part2":
                    layer = args[0]
                    f2, r = (a[:, :, :, :].rearrange("p a t n -> p (a t n)") for a in (part2, rest))
                    settle()
                    nc.vector.tensor_copy(f2, r).then_inc(parts_ready[layer], 1)
                    settle()
                    nc.vector.memset(q_tok[layer][:, :, :, MAX_ROW:MAX_ROW + 2], 0.0)
                    nc.vector.tensor_tensor(q_tok[layer][:, :, :, 4 * HD:5 * HD],
                                            rest[:, 0, :, :].rearrange("p t (h d) -> p t h d", d=HD),
                                            part2[:, 0, :, :].rearrange("p t (h d) -> p t h d", d=HD), ALU.subtract).then_inc(q3_ready[layer], 1)
                elif name == "rows":
                    layer, what, half = args
                    buf, full, _, _ = wide_of(now)
                    dve.wait_ge(wide_full, full)
                    if what == "q":
                        ins = nc.vector.tensor_copy(flat(q_t[layer][:, 4 * half:4 * half + 4, :]), flat(wide[buf][:, :, :]).bitcast(BF16))
                    else:
                        ins = nc.vector.tensor_copy(flat(k_t[layer][ROWS:, 1, 4 * half:4 * half + 4, :]),
                                                    flat(wide[buf][ROWS:, :, :]).bitcast(BF16))
                    ins.then_inc(wide_free[buf], 1)
                elif name == "score":
                    layer, tile = args
                    h, qb = divmod(tile, BLOCKS)
                    width = P * (qb + 1) if layer else TOKENS
                    buf, full, free = score_of(now)
                    dve.wait_ge(score_full, full)
                    nc.vector.tensor_reduce(neg_max[:, layer, qb, h:h + 1], score[buf][:, 0:width], AX.X, ALU.max,
                                            negate=True).then_inc(score_free, 1)
                    if tile % GTILES == GTILES - 1:
                        g = h // GROUP
                        hs = slice(GROUP * g, GROUP * (g + 1))
                        settle()
                        nc.vector.tensor_copy(q_tok[layer][:, :, hs, MAX_ROW], neg_max[:, layer, :, hs])
                        settle()
                        nc.vector.tensor_tensor(q_tok[layer][:, :, hs, MAX_ROW + 1], neg_max[:, layer, :, hs],
                                                q_tok[layer][:, :, hs, MAX_ROW], ALU.subtract).then_inc(max_ready[layer], 1)
                elif name == "group_out":
                    layer, g = args
                    dve.wait_ge(turn_full, turn_of(now)[0])
                    o = turn[:, :].rearrange("p (t j r) -> p t j r", t=BLOCKS, j=GROUP)
                    nc.vector.reciprocal(rec[:, :, :], o[:, :, :, HD])
                    settle()
                    nc.vector.tensor_tensor(att[:, :, GROUP * HD * g:GROUP * HD * (g + 1)].rearrange("p t (j d) -> p t j d", d=HD),
                                            o[:, :, :, 0:HD], rec[:, :, :].unsqueeze(3).broadcast_to([P, BLOCKS, GROUP, HD]),
                                            ALU.mult).then_inc(turn_free, 1)
                elif name == "project":
                    buf, full, free = score_of(now)
                    if args[0] == 0:
                        dve.wait_ge(res1_ready, now.seq(1, 1))
                        if not now.first_seq():
                            dve.wait_ge(kept, now.seq(1, 0))
                        dve.wait_ge(score_full, full)
                        nc.vector.tensor_tensor(x1_new[:, :, :], score[buf][:, :].rearrange("p (t n) -> p t n", t=BLOCKS),
                                                res1[:, :, :], ALU.add).then_inc(score_free, 1)
                    else:
                        dve.wait_ge(kept, now.seq(1, 1))
                        dve.wait_ge(score_full, full)
                        nc.vector.tensor_tensor(y[:, :, KEPT:], score[buf][:, 0:BLOCKS * OUTC].rearrange("p (t n) -> p t n", t=BLOCKS),
                                                y[:, :, KEPT:], ALU.add).then_inc(score_free, 1)
                        settle()
                        nc.vector.memset(credit[:, 0:1], 0.0).then_inc(u_ready, 1)
                elif name == "route" and args[0] == 0:
                    dve.wait_ge(turn_full, router_full(now))
                    nc.vector.tensor_copy(lg[:, :, :], turn[:, 0:BLOCKS * EXPERTS].rearrange("p (t e) -> p t e", e=EXPERTS)).then_inc(turn_free, 1)
                    settle()
                    nc.vector.memset(lgc[:, :, :], 0.0)
                    nc.vector.tensor_tensor(lg_ok[:, :, :], lg[:, :, :], lg[:, :, :], ALU.is_equal)
                    settle()
                    nc.vector.copy_predicated(lgc[:, :, :], lg_ok[:, :, :], lg[:, :, :])
                    settle()
                    nc.vector.tensor_scalar(lg[:, :, :], lgc[:, :, :], -F32_MAX, F32_MAX, ALU.max, ALU.min)
                    settle()
                    nc.vector.tensor_reduce(lmax[:, :], lg[:, :, :], AX.X, ALU.max)
                    settle()
                    nc.vector.tensor_tensor(lgc[:, :, :], lg[:, :, :], lmax[:, :].unsqueeze(2).broadcast_to([P, BLOCKS, EXPERTS]),
                                            ALU.subtract).then_inc(logits_ready, 1)
                elif name == "route":
                    dve.wait_ge(lexp_ready, now.seq(1, 1))
                    four = [P, BLOCKS, EXPERTS, EXPERTS]
                    nc.vector.tensor_reduce(lmax[:, :], lexp[:, :, :], AX.X, ALU.add)
                    settle()
                    nc.vector.reciprocal(lmax[:, :], lmax[:, :])
                    settle()
                    nc.vector.tensor_tensor(prob[:, :, :], lexp[:, :, :], lmax[:, :].unsqueeze(2).broadcast_to([P, BLOCKS, EXPERTS]), ALU.mult)
                    settle()
                    p_i = prob[:, :, :].unsqueeze(2).broadcast_to(four)
                    p_j = prob[:, :, :].unsqueeze(3).broadcast_to(four)
                    nc.vector.tensor_tensor(ahead[:, :, :, :], p_i, p_j, ALU.is_ge)
                    nc.vector.tensor_tensor(ahead2[:, :, :, :], p_i, p_j, ALU.is_gt)
                    settle()
                    nc.vector.tensor_tensor(ahead[:, :, :, :], ahead[:, :, :, :], before[:, :, :].unsqueeze(1).broadcast_to(four), ALU.mult)
                    nc.vector.tensor_tensor(ahead2[:, :, :, :], ahead2[:, :, :, :], behind[:, :, :].unsqueeze(1).broadcast_to(four), ALU.mult)
                    settle()
                    nc.vector.tensor_tensor(ahead[:, :, :, :], ahead[:, :, :, :], ahead2[:, :, :, :], ALU.add)
                    settle()
                    nc.vector.tensor_reduce(rank[:, :, :], ahead[:, :, :, :], AX.X, ALU.add)
                    settle()
                    nc.vector.scalar_tensor_tensor(out=wts[:, :, :], in0=rank[:, :, :], scalar=1.5, in1=prob[:, :, :],
                                                        op0=ALU.is_lt, op1=ALU.mult)
                    settle()
                    nc.vector.tensor_reduce(lmax[:, :], wts[:, :, :], AX.X, ALU.add)
                    settle()
                    nc.vector.tensor_scalar(lmax[:, :], lmax[:, :], 1e-8, None, ALU.add)
                    settle()
                    nc.vector.reciprocal(lmax[:, :], lmax[:, :])
                    settle()
                    nc.vector.tensor_tensor(wts[:, :, :], wts[:, :, :], lmax[:, :].unsqueeze(2).broadcast_to([P, BLOCKS, EXPERTS]), ALU.mult)
                    settle()
                elif name == "expert" and args[0] == 1:
                    buf, full, _, _ = wide_of(now)
                    other, _, _, used = wide_of(now, ("expert", 0))
                    dve.wait_ge(wide_full, full)
                    dve.wait_ge(wide_free[other], used)
                    nc.vector.tensor_tensor(hid["h_e1"], hid["h_e1"], wide[buf][:, :, :], ALU.mult).then_inc(wide_free[buf], 1)
                elif name == "down":
                    k = args[0]
                    buf, full, free = score_of(now)
                    if k == 0:
                        dve.wait_ge(sum_ready, now.seq(1, 1))
                    dve.wait_ge(score_full, full)
                    for e in range(EXPERTS):
                        ins = nc.vector.scalar_tensor_tensor(
                            out=x1[:, k, KEPT:], in0=score[buf][:, OUTC * e:OUTC * (e + 1)], scalar=wts[:, k, e:e + 1],
                            in1=x1[:, k, KEPT:], op0=ALU.mult, op1=ALU.add)
                        if e < EXPERTS - 1:
                            settle()
                    ins.then_inc(score_free, 1)

            NORM = ((x, z), (z, n[0]), (x1_new, y_new), (y_new, n[1]), (y, n[2]))

            def router_full(now):
                first, per = now.fill("turn", ("router",))
                return now.count(first + 1, per)

            walk(dve, part)

        @block.tensor
        def _(pe):
            pe.wait_ge(w_loaded, 16 * W_LOADS)
            pe.wait_ge(consts, 1)
            for u in range(W_SETUP):
                if u >= 2:
                    pe.wait_ge(wide_free[u % 2], u // 2)
                for k in range(8 * u, min(8 * u + 8, NWT)):
                    ins = nc.tensor.transpose(wide[u % 2][:, k % 8 // 4, k % 4 * P:k % 4 * P + P], stage[:, k, :], id_f[:, :])
                ins.then_inc(wide_full, 1)
            nc.tensor.transpose(turn[:, 0:EXPERTS], gate_raw[:, :], id_f[0:EXPERTS, 0:EXPERTS])
            nc.tensor.matmul(turn[:, 128:128 + D + 2 * HD], ones_row[:, :], row[:, :], start=True, stop=True).then_inc(turn_full, 1)
            pe.wait_ge(w_ready, 3)
            pe.wait_ge(consts, 2)

            def by_token(src, now):
                full, free = turn_of(now)
                pe.wait_ge(turn_free, free)
                for k in range(BLOCKS):
                    ins = nc.tensor.transpose(turn[:, P * k:P * (k + 1)], src(k), id_f[:, :])
                ins.then_inc(turn_full, 1)

            def turn_read(now, task):
                first, per = now.fill("turn", task)
                pe.wait_ge(turn_free, now.count(first + 1, per))

            shared = {}

            def written(now, *tasks, fill=False):
                counts = {}
                for task in tasks:
                    first, per = now.fill("wide", task)
                    counts[first % 2] = max(counts.get(first % 2, (0, 0)), (first // 2 + 1, per // 2))
                buf, _, _, _ = wide_of(now) if fill else (None,) * 4
                if fill:
                    first, per = now.fill("wide")
                    counts[buf] = max(counts.get(buf, (0, 0)), (first // 2, per // 2))
                for b, (c, per) in counts.items():
                    pe.wait_ge(wide_free[b], now.count(c, per))
                if fill and buf in shared:
                    pe.wait_ge(*shared.pop(buf))
                return buf

            def wide_wait(now):
                return written(now, fill=True)

            EXPERT_IN = ((E1_W1, 2, None), (E1_W2, 2, None), (E2_L1, 2, None), (E3_DOWN, 1, None), (E2_L2, 2, "h_l1"),
                         (E3_UP, 2, "h_e3d"), (E2_L3, 2, "h_l2"), (E0_UP, 2, None))
            EXPERT_NEEDS = {4: 2, 5: 3, 6: 4}

            def part(now, name, *args):
                if name == "norm_t":
                    w = args[0]
                    pe.wait_ge(n_ready[w], now.seq(1, 1))
                    by_token(lambda k: n[w][:, k, :], now)
                elif name == "qk":
                    layer = args[0]
                    turn_read(now, ("norm_t", layer))
                    buf = wide_wait(now)
                    w_in = wqkv1[:, 0:2, :] if layer == 0 else wt[:, WQKV2:WQKV2 + 2, :]
                    dst = flat(wide[buf][:, :, :])
                    for k in range(BLOCKS):
                        ins = nc.tensor.matmul(dst[:, 2 * D * k:2 * D * (k + 1)], n_t[layer][:, P * k:P * (k + 1)], flat(w_in),
                                               start=True, stop=True)
                    ins.then_inc(wide_full, 1)
                elif name == "v":
                    layer = args[0]
                    turn_read(now, ("norm_t", layer))
                    buf = wide_wait(now)
                    w_in = wqkv1[:, 2, :] if layer == 0 else wt[:, WQKV2 + 2, :]
                    for k in range(BLOCKS):
                        ins = nc.tensor.matmul(wide[buf][:, 0, D * k:D * (k + 1)], n_t[layer][:, P * k:P * (k + 1)], w_in,
                                               start=True, stop=True)
                    ins.then_inc(wide_full, 1)
                elif name == "rows":
                    layer, what, half = args
                    src = k_tok if what == "k" else q_tok[layer]
                    if what == "k":
                        pe.wait_ge(ktok_ready[layer], now.seq(1, 1))
                    else:
                        pe.wait_ge(qtok_ready[layer], now.seq(1, 1))
                        pe.wait_ge(q3_ready[layer], now.seq(1, 1))
                    buf = wide_wait(now)
                    dst = flat(wide[buf][:, :, :]).bitcast(BF16)
                    for a in range(4):
                        pair = 4 * half + a
                        for k in range(BLOCKS):
                            ins = nc.tensor.transpose(dst[:, TOKENS * a + P * k:TOKENS * a + P * (k + 1)],
                                                      src[:, k, 2 * pair:2 * pair + 2, :].rearrange("p h r -> p (h r)"), id_b[:, :])
                    ins.then_inc(wide_full, 1)
                    if what == "k":
                        shared[buf] = (k_even[layer], now.seq(2, half + 1))
                elif name == "score":
                    layer, tile = args
                    h, qb = divmod(tile, BLOCKS)
                    width = P * (qb + 1) if layer else TOKENS
                    if tile == 0:
                        written(now, ("rows", layer, "k", 1), ("rows", layer, "q", 1))
                        pe.wait_ge(k_even[layer], now.seq(2, 2))
                    buf, _, free = score_of(now)
                    pe.wait_ge(score_free, free)
                    ins = nc.tensor.matmul(score[buf][:, 0:width], q_t[layer][:, h // 2, P * qb:P * (qb + 1)],
                                           k_t[layer][:, h % 2, h // 2, 0:width], start=True, stop=not layer)
                    if layer:
                        ins = nc.tensor.matmul(score[buf][:, P * qb:width], id_b[:, :], mask_qk[:, :], start=False, stop=True)
                    ins.then_inc(score_full, 1)
                elif name == "max_rows":
                    layer, g = args
                    pe.wait_ge(max_ready[layer], now.seq(GROUPS, g + 1))
                    pe.wait_ge(turn_free, turn_of(now)[1])
                    dst = turn[:, :].bitcast(BF16)
                    for a in range(2):
                        for k in range(BLOCKS):
                            h = GROUP * g + 2 * a
                            ins = nc.tensor.transpose(dst[:, TOKENS * a + P * k:TOKENS * a + P * (k + 1)],
                                                      q_tok[layer][:, k, h:h + 2, :].rearrange("p h r -> p (h r)"), id_b[:, :])
                    ins.then_inc(turn_full, 1)
                elif name == "shifted":
                    layer, i, half = args
                    g, kb = divmod(i, BLOCKS)
                    if kb == 0 and half == 0:
                        turn_read(now, ("max_rows", layer, g))
                    buf = wide_wait(now)
                    pair = 2 * g + half
                    c0 = P * kb if layer else 0
                    for k in range(2):
                        ins = nc.tensor.matmul(wide[buf][:, k, c0:], k_t[layer][:, k, pair, P * kb:P * (kb + 1)],
                                               q_t[layer][:, pair, c0:], start=True, stop=not layer)
                        if layer:
                            ins = nc.tensor.matmul(wide[buf][:, k, c0:c0 + P], id_b[:, :], mask_kq[:, :], start=False, stop=True)
                    ins.then_inc(wide_full, 1)
                elif name == "values":
                    layer, i = args
                    g, kb = divmod(i, BLOCKS)
                    c0 = P * kb if layer else 0
                    written(now, ("shifted", layer, i, 0), ("shifted", layer, i, 1))
                    first, per = step_of(now, layer, i)
                    if kb == 0 and first > 0:
                        pe.wait_ge(ot_ready, now.count(first // BLOCKS, per // BLOCKS))
                    for j in range(GROUP):
                        ins = nc.tensor.matmul(pv[32 * j:32 * j + 32, c0:], v_one[layer][:, kb, GROUP * g + j, :],
                                               probs[:, i % RING, j, c0:], start=(kb == 0), stop=(kb == BLOCKS - 1),
                                               tile_position=(0, 32 * j))
                    ins.then_inc(pv_done, 1)
                elif name == "group_out":
                    layer, g = args
                    first, per = step_of(now, layer, BLOCKS * g + BLOCKS - 1)
                    pe.wait_ge(ot_ready, now.count(first // BLOCKS + 1, per // BLOCKS))
                    by_token(lambda k: o_t[:, P * k:P * (k + 1)], now)
                elif name == "att_t":
                    turn_read(now, ("group_out", args[0], GROUPS - 1))
                    by_token(lambda k: att[:, k, :], now)
                elif name == "project":
                    layer = args[0]
                    turn_read(now, ("att_t", layer))
                    buf, _, free = score_of(now)
                    pe.wait_ge(score_free, free)
                    width = OUTC if layer else D
                    w_out = wt[:, WO, KEPT:] if layer else wproj[:, :]
                    for k in range(BLOCKS):
                        ins = nc.tensor.matmul(score[buf][:, width * k:width * (k + 1)], att_t[:, P * k:P * (k + 1)], w_out,
                                               start=True, stop=True)
                    ins.then_inc(score_full, 1)
                elif name == "router":
                    pe.wait_ge(turn_free, turn_of(now)[1])
                    for k in range(BLOCKS):
                        ins = nc.tensor.matmul(turn[:, EXPERTS * k:EXPERTS * (k + 1)], n_t[2][:, P * k:P * (k + 1)], gate_t[:, :],
                                               start=True, stop=True)
                    ins.then_inc(turn_full, 1)
                elif name == "expert":
                    u = args[0]
                    at, halves, src = EXPERT_IN[u]
                    srcs = {None: lambda: [n_t[2][:, :]], "h_e3d": lambda: [h_e3d[:, :]]}.get(
                        src, lambda: [hid[src][:, k, :] for k in range(2)])()
                    buf = written(now, *((("expert", EXPERT_NEEDS[u]),) if u in EXPERT_NEEDS else ()), fill=True)
                    for a in range(halves):
                        for k, moving in enumerate(srcs):
                            ins = nc.tensor.matmul(wide[buf][:, a, :], wt[:, at + len(srcs) * a + k, :], moving,
                                                   start=(k == 0), stop=(k == len(srcs) - 1))
                    ins.then_inc(wide_full, 1)
                elif name == "down":
                    k = args[0]
                    if k == 0:
                        written(now, *(("expert", u) for u in (1, 5, 6, 7)))
                    buf, _, free = score_of(now)
                    pe.wait_ge(score_free, free)
                    for e, (at, source) in enumerate(((E0_DN, "h_e0"), (E1_DN, "h_e1"), (E2_DN, "h_l3"), (E3_DN, "h_e3"))):
                        for a in range(2):
                            ins = nc.tensor.matmul(score[buf][:, OUTC * e:OUTC * (e + 1)], hid[source][:, a, P * k:P * (k + 1)],
                                                   wt[:, at + a, KEPT:], start=(a == 0), stop=(a == 1))
                    ins.then_inc(score_full, 1)

            walk(pe, part)


_INS = ['L0_attn_z', 'L0_attn_ln_scale', 'L0_attn_ln_bias', 'L0_attn_w_qkv', 'L0_attn_w_proj', 'L0_attn_b_proj', 'L0_ffn_n1_w',
        'L0_ffn_n2_w', 'L0_ffn_wq', 'L0_ffn_wk', 'L0_ffn_wv', 'L0_ffn_wo', 'L0_ffn_qn_w', 'L0_ffn_kn_w', 'L0_ffn_gate_w',
        'L0_ffn_e0_up', 'L0_ffn_e0_down', 'L0_ffn_e1_w1', 'L0_ffn_e1_w2', 'L0_ffn_e1_down', 'L0_ffn_e2_l1', 'L0_ffn_e2_l2',
        'L0_ffn_e2_l3', 'L0_ffn_e2_l4', 'L0_ffn_e3_down', 'L0_ffn_e3_up', 'L0_ffn_e3_out']


def kernel(**inputs):
    import numpy as _np
    import concourse.bacc as _bacc
    from concourse import mybir as _mybir
    from concourse.bass_utils import run_bass_kernel_spmd as _run

    nc = _bacc.Bacc("TRN2", target_bir_lowering=False, num_devices=1)
    arrays, args = {}, {}
    for name in _INS:
        a = _np.ascontiguousarray(inputs[name])
        arrays[f"in_{name}_dram"] = a
        args[name] = nc.dram_tensor(f"in_{name}_dram", a.shape, _mybir.dt.from_np(a.dtype), kind="ExternalInput").ap()
    result = nc.dram_tensor("out_0_dram", (SEQS, TOKENS, D), F32, kind="ExternalOutput").ap()
    program(nc, args, result)
    r = _run(nc, [arrays], core_ids=[0])
    return r.results[0]["out_0_dram"]
```
